# Optimizing a Trainium2 kernel written in Bass

```python
import numpy as np
import jax
import jax.numpy as jnp

def _softmax(x, axis=-1):
    return jax.nn.softmax(x, axis=axis)

def _gelu(x):
    return jax.nn.gelu(x, approximate=True)

def _silu(x):
    return jax.nn.silu(x)

def _sigmoid(x):
    return jax.nn.sigmoid(x)

def _layernorm(x, axis=-1, eps=1e-05):
    m = jnp.mean(x, axis=axis, keepdims=True)
    v = jnp.var(x, axis=axis, keepdims=True)
    return (x - m) / jnp.sqrt(v + eps)

def _scatter_add(tgt, idx, src, axis=0):
    return tgt.at[idx].add(src)

def _segment_sum(src, seg, n):
    return jax.ops.segment_sum(src, seg, n)
kernel_name = 'mk_vit_tower_d1_tok_img1024_r4_432049'

def setup_inputs(seed: int=0):
    np.random.seed(seed)
    _w = jnp.asarray

    def _rec_inputs():
        import jax
        import jax.numpy as jnp
        _rk = jax.random.key(seed)
        x = -0.000125008 + 0.999885 * jax.random.normal(jax.random.fold_in(_rk, 1), (4, 512, 256, 4), jnp.float32)
        return x
    x = _rec_inputs()

    def _L0_tok_setup():
        import jax, jax.numpy as jnp
        import numpy as np
        key = jax.random.key(seed)
        k1, k2, k3 = jax.random.split(key, 3)
        B, H, I, O, Dp1 = (4, 512, 256, 256, 4)
        x = jax.random.normal(k1, (B, H, I, Dp1), dtype=jnp.float32)
        weight = 0.1 * jax.random.normal(k2, (O, Dp1), dtype=jnp.float32)
        weighted_sum = 0.1 * jax.random.normal(k3, (O, I), dtype=jnp.float32)
        return {'x': x, 'weight': weight, 'weighted_sum': weighted_sum}
    _L0_tok_all = _L0_tok_setup()
    _L0_tok_in = {k: v for k, v in _L0_tok_all.items() if k in ('weight', 'weighted_sum')}
    del _L0_tok_all

    def _L0_attn_setup():
        import jax, jax.numpy as jnp
        import numpy as np
        DIM = 256
        HEADS = 16
        HIDDEN = 512
        EPS = 1e-06

        def _rmsnorm(x, scale):
            norm = jnp.linalg.norm(x, axis=-1, keepdims=True)
            return x * (scale * (x.shape[-1] ** 0.5 + EPS) / norm)
        key = jax.random.key(seed)
        ks = jax.random.split(key, 8)
        B, N, C = (4, 1024, DIM)
        s = 0.02
        return {'x': jax.random.normal(ks[0], (B, N, C), dtype=jnp.float32), 'scale1': jnp.ones((C,), jnp.float32), 'scale2': jnp.ones((C,), jnp.float32), 'gamma': jnp.ones((C,), jnp.float32), 'qkv_w': jax.random.normal(ks[1], (3 * C, C), jnp.float32) * s, 'proj_w': jax.random.normal(ks[2], (C, C), jnp.float32) * s, 'proj_b': jnp.zeros((C,), jnp.float32), 'conv1_w': jax.random.normal(ks[3], (HIDDEN, C), jnp.float32) * s, 'conv1_b': jnp.zeros((HIDDEN,), jnp.float32), 'conv2_w': jax.random.normal(ks[4], (C, HIDDEN), jnp.float32) * s, 'conv2_b': jnp.zeros((C,), jnp.float32)}
    _L0_attn_all = _L0_attn_setup()
    _L0_attn_in = {k: v for k, v in _L0_attn_all.items() if k in ('scale1', 'scale2', 'gamma', 'qkv_w', 'proj_w', 'proj_b', 'conv1_w', 'conv1_b', 'conv2_w', 'conv2_b')}
    del _L0_attn_all

    def _L0_ffn_setup():
        import jax, jax.numpy as jnp
        import numpy as np
        B, N, D = (4, 512, 256)
        SPARSITY = 0.01
        key = jax.random.key(seed)
        k1, k2, k3 = jax.random.split(key, 3)
        x = jax.random.normal(k1, (B, N, D), dtype=jnp.float32)
        spatial = jax.random.normal(k2, (D, D), dtype=jnp.float32) * 0.02
        freq = jnp.fft.fft(spatial, axis=-1)
        k = int(D * SPARSITY)
        mag = jnp.abs(freq)
        kth = jax.lax.top_k(mag, k)[0][:, -1:]
        w_sparse = jnp.where(mag >= kth, freq, 0.0 + 0j)
        bias = jax.random.normal(k3, (D,), dtype=jnp.float32) * 0.01
        return {'x': x, 'w_freq_real': jnp.real(w_sparse).astype(jnp.float32), 'w_freq_imag': jnp.imag(w_sparse).astype(jnp.float32), 'bias': bias}
    _L0_ffn_all = _L0_ffn_setup()
    _L0_ffn_in = {k: v for k, v in _L0_ffn_all.items() if k in ('w_freq_real', 'w_freq_imag', 'bias')}
    del _L0_ffn_all
    return {'x': x, 'L0_tok_weight': _L0_tok_in['weight'], 'L0_tok_weighted_sum': _L0_tok_in['weighted_sum'], 'L0_attn_scale1': _L0_attn_in['scale1'], 'L0_attn_scale2': _L0_attn_in['scale2'], 'L0_attn_gamma': _L0_attn_in['gamma'], 'L0_attn_qkv_w': _L0_attn_in['qkv_w'], 'L0_attn_proj_w': _L0_attn_in['proj_w'], 'L0_attn_proj_b': _L0_attn_in['proj_b'], 'L0_attn_conv1_w': _L0_attn_in['conv1_w'], 'L0_attn_conv1_b': _L0_attn_in['conv1_b'], 'L0_attn_conv2_w': _L0_attn_in['conv2_w'], 'L0_attn_conv2_b': _L0_attn_in['conv2_b'], 'L0_ffn_w_freq_real': _L0_ffn_in['w_freq_real'], 'L0_ffn_w_freq_imag': _L0_ffn_in['w_freq_imag'], 'L0_ffn_bias': _L0_ffn_in['bias']}

def reference(x, L0_tok_weight, L0_tok_weighted_sum, L0_attn_scale1, L0_attn_scale2, L0_attn_gamma, L0_attn_qkv_w, L0_attn_proj_w, L0_attn_proj_b, L0_attn_conv1_w, L0_attn_conv1_b, L0_attn_conv2_w, L0_attn_conv2_b, L0_ffn_w_freq_real, L0_ffn_w_freq_imag, L0_ffn_bias):
    import jax
    import jax.numpy as jnp

    def _L0_tok_ref(x, weight, weighted_sum):
        import jax, jax.numpy as jnp
        import numpy as np
        return jnp.einsum('bhid,oi,od->bho', x, weighted_sum, weight)

    def _L0_attn_ref(x, scale1, scale2, gamma, qkv_w, proj_w, proj_b, conv1_w, conv1_b, conv2_w, conv2_b):
        import jax, jax.numpy as jnp
        import numpy as np
        DIM = 256
        HEADS = 16
        HIDDEN = 512
        EPS = 1e-06

        def _rmsnorm(x, scale):
            norm = jnp.linalg.norm(x, axis=-1, keepdims=True)
            return x * (scale * (x.shape[-1] ** 0.5 + EPS) / norm)
        B, N, C = x.shape
        h, d = (HEADS, C // HEADS)
        xn = _rmsnorm(x, scale1)
        qkv = jnp.einsum('bnc,fc->bnf', xn, qkv_w)
        qkv = qkv.reshape(B, N, 3, h, d).transpose(2, 0, 3, 1, 4)
        q, k, v = (qkv[0], qkv[1], qkv[2])
        phi = lambda t: jnp.exp(-0.5 * t * t)
        q, k = (phi(q), phi(k))
        kv = jnp.einsum('bhnd,bhne->bhde', k, v)
        z = 1.0 / (jnp.einsum('bhnd,bhd->bhn', q, k.sum(2)) + 1e-06)
        out = jnp.einsum('bhnd,bhde,bhn->bhne', q, kv, z)
        out = out.transpose(0, 2, 1, 3).reshape(B, N, C)
        attn = jnp.einsum('bnc,oc->bno', out, proj_w) + proj_b
        x = x + gamma * attn
        xn2 = _rmsnorm(x, scale2)
        hdd = jax.nn.gelu(jnp.einsum('bnc,hc->bnh', xn2, conv1_w) + conv1_b, approximate=False)
        mlp = jnp.einsum('bnh,ch->bnc', hdd, conv2_w) + conv2_b
        return x + gamma * mlp

    def _L0_ffn_ref(x, w_freq_real, w_freq_imag, bias):
        import jax, jax.numpy as jnp
        import numpy as np
        B, N, D = (4, 512, 256)
        SPARSITY = 0.01
        w = jax.lax.complex(w_freq_real, w_freq_imag)
        x_freq = jnp.fft.fft(x, axis=-1)
        y_freq = jnp.einsum('bnd,do->bno', x_freq, w)
        y = jnp.real(jnp.fft.ifft(y_freq, axis=-1))
        return y + bias
    h = _L0_tok_ref(x, L0_tok_weight, L0_tok_weighted_sum)
    h = h + _L0_attn_ref(_layernorm(h, axis=-1), L0_attn_scale1, L0_attn_scale2, L0_attn_gamma, L0_attn_qkv_w, L0_attn_proj_w, L0_attn_proj_b, L0_attn_conv1_w, L0_attn_conv1_b, L0_attn_conv2_w, L0_attn_conv2_b)
    h = h + _L0_ffn_ref(_layernorm(h, axis=-1), L0_ffn_w_freq_real, L0_ffn_w_freq_imag, L0_ffn_bias)
    return h

_drawn_inputs = setup_inputs


def setup_inputs(seed=0):
    import zlib

    import numpy as np

    out = dict(_drawn_inputs(seed))
    spreads = {'L0_attn_scale1': (1.0, 0.6),
     'L0_attn_scale2': (1.0, 0.6),
     'L0_attn_gamma': (1.0, 0.547),
     'L0_attn_proj_b': (0.0, 0.1),
     'L0_attn_conv1_b': (0.0, 0.431),
     'L0_attn_conv2_b': (0.0, 0.1)}
    factors = {'L0_attn_qkv_w': 8.0, 'L0_attn_proj_w': 8.0, 'L0_ffn_bias': 8.0}
    for name, (base, spread) in spreads.items():
        noise = np.random.default_rng([zlib.crc32(name.encode()), seed]).standard_normal(out[name].shape)
        drawn = base * np.exp(spread * noise) if base else spread * noise
        out[name] = jnp.asarray(drawn.astype(out[name].dtype))
    for name, factor in factors.items():
        out[name] = (out[name] * factor).astype(out[name].dtype)
    return out
```

```python
from contextlib import ExitStack

import concourse.bass as bass
from concourse import mybir

F32 = mybir.dt.float32
F32R = mybir.dt.float32r
ALU = mybir.AluOpType
ACT = mybir.ActivationFunctionType

P = 128
B = 4
T = 512
TT = T // P
C = 256
CH = C // P
D = 4
HID = 512
HT = HID // P
DH = 16
HPH = P // DH
LN_EPS = 1e-5
RMS_GAIN = C ** 0.5 + 1e-6
DEN_EPS = 1e-6
V_SCALE1, V_SCALE2, V_GAMMA, V_PROJB, V_CONV2B, V_FFNB, V_CONV1B, V_END = 0, 2, 4, 6, 8, 10, 12, 16
TOK_BANK = 0
MEAN1_BANK, STAT_BANK, RNORM_BANK, RSTD_BANK = 2, 3, 4, 5
DFT_U_BANK, DFT_V_BANK = 6, 7
QKV_BANKS = (0, 1, 6, 7)
KV_BANK = 2
Z_BANK = 4
RMS_BANK = 0
CONV1_BANK = 6
FFN_BANKS = (0, 2)
CONV2_BANK = 4
MEAN2_BANKS = (1, 1, 6, 6)
RSTD2_BANK = 1
DFT_M_BANK = 2
DEN_COL, SS1_COL, SS2_COL, SS3_COL = 0, 64, 72, 80


def build(nc, x, ws, w, vec, qkv_w, proj_w, conv1_w, conv2_w, dft, freq, out):
    with ExitStack() as ctx:
        def sb(name, shape, dt=F32):
            return ctx.enter_context(nc.sbuf_tensor(name, shape, dt))

        def sem(name):
            return ctx.enter_context(nc.semaphore(name))

        x_ring = sb("x_ring", [P, D, CH * T])
        xhi_ring = sb("xhi_ring", [P, D, CH * T], F32R)
        xlo_ring = sb("xlo_ring", [P, D, CH * T], F32R)
        late = x_ring[:, :, :].rearrange("p a n -> p (a n)")
        g = late[:, 0:HT * T].rearrange("p (j n) -> p j n", j=HT)
        sq2 = late[:, HT * T:(HT + CH) * T].rearrange("p (c n) -> p c n", c=CH)
        xn2 = late[:, (HT + CH) * T:(HT + 2 * CH) * T].rearrange("p (c n) -> p c n", c=CH)
        ghi = xhi_ring[:, :, :].rearrange("p a n -> p (a n)").rearrange("p (r j n) -> p r j n", r=2, j=HT)
        glo = xlo_ring[:, :, :].rearrange("p a n -> p (a n)").rearrange("p (r j n) -> p r j n", r=2, j=HT)
        fout = (xn2, sq2)
        wtok = sb("wtok", [P, D, CH * C])
        wtok_hi = sb("wtok_hi", [P, D, CH * C], F32R)
        wtok_lo = sb("wtok_lo", [P, D, CH * C], F32R)
        stage = wtok[:, :, :].rearrange("p a n -> p (a n)")
        q = wtok[:, :, :].rearrange("p a n -> p (a n)").rearrange("p (r c n) -> p r c n", r=2, c=CH)
        qz_hi = wtok_hi[:, :, :].rearrange("p a n -> p (a n)").rearrange("p (r c n) -> p r c n", r=2, c=CH)
        qz_lo = wtok_lo[:, :, :].rearrange("p a n -> p (a n)").rearrange("p (r c n) -> p r c n", r=2, c=CH)
        k = sb("k", [P, 2, TT, C])
        v = sb("v", [P, 2, TT, CH, P + 1])
        dft_sb = k[:, 0].rearrange("p t n -> p (t n)").rearrange("p (a c n) -> p a c n", a=2, c=CH)
        freq_sb = k[:, 1].rearrange("p t n -> p (t n)").rearrange("p (a c n) -> p a c n", a=2, c=CH)
        uv = v[:, 0].rearrange("p t c n -> p (t c n)")[:, 0:2 * CH * C].rearrange("p (a c n) -> p a c n", a=2, c=CH)
        w_bc = v[:, 1].rearrange("p t c n -> p (t c n)")[:, 0:D * C].rearrange("p (d o) -> p d o", d=D)
        h = sb("h", [P, CH, B * T])
        u = sb("u", [P, CH, B * T])
        xn_hi = sb("xn_hi", [P, B, CH, T], F32R)
        xn_lo = sb("xn_lo", [P, B, CH, T], F32R)
        hsum = sb("hsum", [P, T])
        ws_sb = hsum
        hc = sb("hc", [P, CH, T])
        sq = sb("sq", [P, CH, T])
        zx = sq[:].rearrange("p c n -> p (c n)")
        qkv_hi = sb("qkv_hi", [P, CH, 3 * C], F32R)
        qkv_lo = sb("qkv_lo", [P, CH, 3 * C], F32R)
        proj = sb("proj", [P, CH, C])
        c1_hi = sb("c1_hi", [P, CH, HID], F32R)
        c1_lo = sb("c1_lo", [P, CH, HID], F32R)
        c2_hi = sb("c2_hi", [P, HT, C], F32R)
        c2_lo = sb("c2_lo", [P, HT, C], F32R)
        m_hi = sb("m_hi", [P, CH, C], F32R)
        m_lo = sb("m_lo", [P, CH, C], F32R)
        vecs = sb("vecs", [P, V_END])
        gain = sb("gain", [P, 4])
        gbias = sb("gbias", [P, 4])
        ident = sb("ident", [P, P])
        mean_w = sb("mean_w", [P, P])
        ones = sb("ones", [P, 1])
        headmask = sb("headmask", [P, P])
        kv_masked = sb("kv_masked", [P, CH, P])
        kvt = sb("kvt", [P, CH, P])
        neg_b = sb("neg_b", [P, T])
        neg_b_sb = neg_b[:].rearrange("p (c n) -> p c n", c=CH)
        row_sum = sb("row_sum", [P, 2, CH])
        row_mean = sb("row_mean", [P, 2, CH])
        ksum_masked = sb("ksum_masked", [P, CH, HPH])
        g_hi = sb("g_hi", [P, CH, C], F32R)
        g_lo = sb("g_lo", [P, CH, C], F32R)
        den = sb("den", [P, TT * CH * HPH])
        z = sb("z", [P, TT * CH * HPH])
        minus_half = sb("minus_half", [P, 2 * TT])
        st1 = sb("st1", [P, 2 * TT])
        rn1 = sb("rn1", [P, 2 * TT])
        st2 = sb("st2", [P, TT])
        rn2 = sb("rn2", [P, TT])
        st3 = sb("st3", [P, TT])
        rn3 = sb("rn3", [P, TT])
        ps = ctx.enter_context(nc.psum_tensor("ps", [P, 8, T], F32))

        def tok(t, b):
            return t[:, :, b * T:(b + 1) * T]

        x_in = [sem(f"x_in{s}") for s in range(D)]
        w_rest_in = sem("w_rest_in")
        ws_in, w_in, vec_in, qkv_in, proj_in, c1_in, c2_in, dft_in = (
            sem(n) for n in ("ws_in", "w_in", "vec_in", "qkv_in", "proj_in", "c1_in", "c2_in", "dft_in"))
        out_sent = sem("out_sent")
        v_ones, kvt_done, kvt_ready, sqsum1_ready, sqsum2_ready, sqsum3_ready, ffn_taken, scaled = (
            sem(n) for n in ("v_ones", "kvt_done", "kvt_ready", "sqsum1_ready", "sqsum2_ready", "sqsum3_ready",
                             "ffn_taken", "scaled"))
        consts_ready, id_zeroed, mask_step, gains_ready = (
            sem(n) for n in ("consts_ready", "id_zeroed", "mask_step", "gains_ready"))
        wtok_ready, wtok_hi_ready, wtok_lo_ready = sem("wtok_ready"), sem("wtok_hi_ready"), sem("wtok_lo_ready")
        xhi_ready, xlo_ready, tok_half0, tok_chunk, h_ready = (
            sem(n) for n in ("xhi_ready", "xlo_ready", "tok_half0", "tok_chunk", "h_ready"))
        wscaled, whi_ready, wlo_ready = sem("wscaled"), sem("whi_ready"), sem("wlo_ready")
        negb_ready, uv_done, uv_raw, uv_sum, uv_mean, uv_ready, m_done, mhi_ready, mlo_ready = (
            sem(n) for n in ("negb_ready", "uv_done", "uv_raw", "uv_sum", "uv_mean", "uv_ready", "m_done", "mhi_ready", "mlo_ready"))
        hsum1_ready, mean1_done, hc1_ready, sq1_ready, ss1_done, st1_ready, rn1_ready, bc1_done = (
            sem(n) for n in ("hsum1_ready", "mean1_done", "hc1_ready", "sq1_ready", "ss1_done", "st1_ready",
                             "rn1_ready", "bc1_done"))
        u_ready, xn_ready, ub_ready, xnhi_ready, xnlo_ready = (
            sem(n) for n in ("u_ready", "xn_ready", "ub_ready", "xnhi_ready", "xnlo_ready"))
        qkv_done, ksq_ready, qsq_ready, k_ready, q_ready, v_ready = (
            sem(n) for n in ("qkv_done", "ksq_ready", "qsq_ready", "k_ready", "q_ready", "v_ready"))
        kv_done, kvm_ready, den_done, den_ready, z_ready, zx_ready, zt_done = (
            sem(n) for n in ("kv_done", "kvm_ready", "den_done", "den_ready", "z_ready", "zx_ready", "zt_done"))
        g_done, ghi_ready, glo_ready, qz_ready, qzhi_ready, qzlo_ready, attn_done, x1_ready = (
            sem(n) for n in ("g_done", "ghi_ready", "glo_ready", "qz_ready", "qzhi_ready", "qzlo_ready",
                             "attn_done", "x1_ready"))
        sq2_ready, ss2_done, st2_ready, rn2_ready, bc2_done, xn2_ready, xn2hi_ready, xn2lo_ready, hx_ready = (
            sem(n) for n in ("sq2_ready", "ss2_done", "st2_ready", "rn2_ready", "bc2_done", "xn2_ready",
                             "xn2hi_ready", "xn2lo_ready", "hx_ready"))
        c1_done, gelu_ready, gehi_ready, gelo_ready, c2_done, h1_ready = (
            sem(n) for n in ("c1_done", "gelu_ready", "gehi_ready", "gelo_ready", "c2_done", "h1_ready"))
        hsum3_ready, mean3_done, hc3_ready, sq3_ready, ss3_done, st3_ready, rn3_ready, bc3_done = (
            sem(n) for n in ("hsum3_ready", "mean3_done", "hc3_ready", "sq3_ready", "ss3_done", "st3_ready",
                             "rn3_ready", "bc3_done"))
        n_ready, nhi_ready, nlo_ready, ffn_done, out_ready = (
            sem(n) for n in ("n_ready", "nhi_ready", "nlo_ready", "ffn_done", "out_ready"))

        QKV, CONV1, CONV2 = range(3)

        block = ctx.enter_context(nc.Block())

        @block.sync
        def _(sp):
            def load_x(b, d):
                if b >= 1:
                    sp.wait_ge(xlo_ready, D * (b - 1) + d + 1)
                sp.dma_start(x_ring[:, d, :], x[b, d]).then_inc(x_in[d], 16)

            sp.dma_start(ws_sb[:], ws).then_inc(ws_in, 16)
            sp.dma_start(w_bc[:, 0:1, :].rearrange("p d o -> p (d o)"), w[:, 0:C]).then_inc(w_in, 16)
            load_x(0, 0)
            sp.dma_start(w_bc[:, 1:D, :].rearrange("p d o -> p (d o)"), w[:, C:D * C]).then_inc(w_rest_in, 16)
            for d in range(1, D):
                load_x(0, d)
            sp.dma_start(vecs[:], vec).then_inc(vec_in, 16)
            for d in range(D):
                load_x(1, d)
            sp.wait_ge(wtok_lo_ready, D)
            sp.dma_start(stage[:, 0:CH * 3 * C], qkv_w).then_inc(qkv_in, 16)
            sp.dma_start(dft_sb.rearrange("p a c n -> p (a c n)"), dft).then_inc(dft_in, 16)
            sp.dma_start(freq_sb.rearrange("p a c n -> p (a c n)"), freq).then_inc(dft_in, 16)
            sp.dma_start(proj[:].rearrange("p c n -> p (c n)"), proj_w).then_inc(proj_in, 16)
            for d in range(D):
                load_x(2, d)
            sp.wait_ge(wlo_ready, QKV + 1)
            sp.dma_start(stage[:, 0:CH * HID], conv1_w).then_inc(c1_in, 16)
            for d in range(D):
                load_x(3, d)
            sp.wait_ge(wlo_ready, CONV1 + 1)
            sp.dma_start(stage[:, 0:HT * C], conv2_w).then_inc(c2_in, 16)
            for b in range(B):
                for o in range(CH):
                    sp.wait_ge(out_ready, CH * b + o + 1)
                    sp.dma_start(out[o, :, b * T:(b + 1) * T], h[:, o, b * T:(b + 1) * T]).then_inc(out_sent, 16)
            sp.wait_ge(out_sent, 16 * CH * B)

        @block.tensor
        def _(pe):
            def split_mm(bank_ap, w_hi, w_lo, m_hi_, m_lo_, first, last):
                nc.tensor.matmul(bank_ap, w_hi, m_hi_, start=first, stop=False)
                nc.tensor.matmul(bank_ap, w_lo, m_hi_, start=False, stop=False)
                return nc.tensor.matmul(bank_ap, w_hi, m_lo_, start=False, stop=last)

            def tok_mix(b, d):
                if b == 0:
                    pe.wait_ge(wtok_lo_ready, d + 1)
                pe.wait_ge(xlo_ready, D * b + d + 1)
                for o in range(CH):
                    if b >= 1 and d == 0:
                        pe.wait_ge(h_ready, CH * (b - 1) + o + 1)
                    for i in range(CH):
                        wc = slice(i * C + o * P, i * C + o * P + P)
                        mm = split_mm(ps[:, TOK_BANK + o, :], wtok_hi[:, d, wc], wtok_lo[:, d, wc],
                                      xhi_ring[:, d, i * T:(i + 1) * T], xlo_ring[:, d, i * T:(i + 1) * T],
                                      d == 0 and i == 0, d == D - 1 and i == CH - 1)
                    if d == D - 1 and o == 0:
                        mm.then_inc(tok_half0, 1)
                mm.then_inc(tok_chunk, 1)

            def square_sums(b, squares, ready, col, done):
                pe.wait_ge(ready, b + 1)
                for t in range(TT):
                    mm = nc.tensor.matmul(ps[:, STAT_BANK, col + t:col + t + 1], squares[:, 0, t * P:(t + 1) * P],
                                          ones[:, 0:1], start=True, stop=True)
                mm.then_inc(done, 1)

            def broadcast(bank, per_token):
                for t in range(TT):
                    mm = nc.tensor.transpose(ps[:, bank, t * P:(t + 1) * P],
                                             per_token[:, t:t + 1].to_broadcast([P, P]), ident[:])
                return mm

            def bc1(b):
                pe.wait_ge(rn1_ready, 2 * b + 1)
                if b >= 1:
                    pe.wait_ge(xn_ready, b)
                broadcast(RNORM_BANK, rn1[:, 0:TT]).then_inc(bc1_done, 1)
                pe.wait_ge(rn1_ready, 2 * b + 2)
                if b >= 1:
                    pe.wait_ge(u_ready, b)
                broadcast(RSTD_BANK, rn1[:, TT:2 * TT]).then_inc(bc1_done, 1)

            def bc2(b):
                pe.wait_ge(rn2_ready, b + 1)
                if b >= 1:
                    pe.wait_ge(xn2_ready, b)
                else:
                    pe.wait_ge(v_ready, TT * (B - 1) + 3)
                broadcast(RMS_BANK, rn2[:]).then_inc(bc2_done, 1)

            def bc3(b):
                pe.wait_ge(rn3_ready, b + 1)
                if b >= 2:
                    pe.wait_ge(scaled, b)
                broadcast(RSTD2_BANK, rn3[:]).then_inc(bc3_done, 1)

            def dft_uv(n):
                pe.wait_ge(negb_ready, 1)
                for m in range(CH):
                    for s, (a, f) in enumerate((((0, 0), (1, 1)), ((0, 1), (2, 0)))[n]):
                        src = freq_sb[:, a] if a < 2 else neg_b_sb
                        for c in range(CH):
                            mm = nc.tensor.matmul(ps[:, DFT_U_BANK + n, m * C:(m + 1) * C],
                                                  src[:, c, m * P:(m + 1) * P], dft_sb[:, f, c, :],
                                                  start=(s == 0 and c == 0), stop=(s == 1 and c == CH - 1))
                mm.then_inc(uv_done, 1)

            def dft_m():
                pe.wait_ge(uv_ready, 2)
                pe.wait_ge(hc1_ready, B)
                for m in range(CH):
                    for f in range(2):
                        for c in range(CH):
                            mm = nc.tensor.matmul(ps[:, DFT_M_BANK, m * C:(m + 1) * C], uv[:, f, c, m * P:(m + 1) * P],
                                                  dft_sb[:, f, c, :], start=(f == 0 and c == 0),
                                                  stop=(f == 1 and c == CH - 1))
                mm.then_inc(m_done, 1)

            def qkv(b, j):
                n = (TT + CH) * b + j
                bank = QKV_BANKS[n % 4]
                if j == 0:
                    pe.wait_ge(xnlo_ready, b + 1)
                if n == 0:
                    pe.wait_ge(wlo_ready, QKV + 1)
                if n < 2:
                    pe.wait_ge(h_ready, CH * (B - 1) + n + 1)
                elif n < 4:
                    pe.wait_ge(uv_raw, n - 1)
                else:
                    pb, pj = divmod(n - 4, TT + CH)
                    if pj < TT:
                        pe.wait_ge(v_ready, TT * pb + pj + 1)
                    else:
                        pe.wait_ge(qsq_ready, CH * pb + pj - TT + 1)
                for c in range(CH):
                    if j < TT:
                        rows = slice(j * P, (j + 1) * P)
                        nc.tensor.matmul(ps[:, bank, :], xn_hi[:, b, c, rows], qkv_hi[:, c, C:3 * C],
                                         start=(c == 0), stop=False)
                        nc.tensor.matmul(ps[:, bank, :], xn_hi[:, b, c, rows], qkv_lo[:, c, C:3 * C],
                                         start=False, stop=False)
                        mm = nc.tensor.matmul(ps[:, bank, :], xn_lo[:, b, c, rows], qkv_hi[:, c, C:3 * C],
                                              start=False, stop=(c == CH - 1))
                    else:
                        o = slice((j - TT) * P, (j - TT + 1) * P)
                        mm = split_mm(ps[:, bank, :], qkv_hi[:, c, o], qkv_lo[:, c, o], xn_hi[:, b, c, :],
                                      xn_lo[:, b, c, :], c == 0, c == CH - 1)
                mm.then_inc(qkv_done, 1)

            def kv(b):
                pe.wait_ge(k_ready, b + 1)
                pe.wait_ge(v_ready, TT * (b + 1))
                if b == 0:
                    pe.wait_ge(mlo_ready, 1)
                    pe.wait_ge(v_ones, 2)
                else:
                    pe.wait_ge(glo_ready, b)
                r = b % 2
                for c in range(CH):
                    for t in range(TT):
                        mm = nc.tensor.matmul(ps[:, KV_BANK, c * (P + 1):(c + 1) * (P + 1)],
                                              k[:, r, t, c * P:(c + 1) * P], v[:, r, t, c, :],
                                              start=(t == 0), stop=(t == TT - 1))
                mm.then_inc(kv_done, 1)

            def kv_turn(b):
                pe.wait_ge(kvm_ready, b + 1)
                for c in range(CH):
                    mm = nc.tensor.transpose(ps[:, KV_BANK, c * P:(c + 1) * P], kv_masked[:, c, :], ident[:])
                mm.then_inc(kvt_done, 1)

            def denominators(b):
                pe.wait_ge(kvm_ready, b + 1)
                pe.wait_ge(q_ready, b + 1)
                if b == 0:
                    pe.wait_ge(st1_ready, B)
                elif b == 1:
                    pe.wait_ge(den_ready, 1)
                else:
                    pe.wait_ge(st2_ready, b - 1)
                for t in range(TT):
                    for c in range(CH):
                        col = DEN_COL + (t * CH + c) * HPH
                        mm = nc.tensor.matmul(ps[:, STAT_BANK, col:col + HPH], q[:, b % 2, c, t * P:(t + 1) * P],
                                              ksum_masked[:, c, :], start=True, stop=True)
                mm.then_inc(den_done, 1)

            def z_channels(b):
                pe.wait_ge(zx_ready, b + 1)
                if b == 0:
                    pe.wait_ge(xn_ready, B)
                    pe.wait_ge(u_ready, B)
                else:
                    pe.wait_ge(x1_ready, CH * b)
                for c in range(CH):
                    for t in range(TT):
                        mm = nc.tensor.transpose(ps[:, Z_BANK + c, t * P:(t + 1) * P],
                                                 zx[:, (t * CH + c) * P:(t * CH + c + 1) * P], ident[:])
                mm.then_inc(zt_done, 1)

            def kv_proj(b):
                pe.wait_ge(kvt_ready, b + 1)
                if b == 0:
                    pe.wait_ge(proj_in, 16)
                for c in range(CH):
                    mm = nc.tensor.matmul(ps[:, KV_BANK, c * C:(c + 1) * C], kvt[:, c, :], proj[:, c, :],
                                          start=True, stop=True)
                mm.then_inc(g_done, 1)

            def attention(b):
                pe.wait_ge(glo_ready, b + 1)
                pe.wait_ge(ghi_ready, b + 1)
                pe.wait_ge(qzlo_ready, b + 1)
                for o in range(CH):
                    for c in range(CH):
                        cols = slice(o * P, (o + 1) * P)
                        mm = split_mm(ps[:, Z_BANK + o, :], g_hi[:, c, cols], g_lo[:, c, cols],
                                      qz_hi[:, b % 2, c, :], qz_lo[:, b % 2, c, :], c == 0, c == CH - 1)
                    mm.then_inc(attn_done, 1)

            def conv1(b, j):
                n = HT * b + j
                if j == 0:
                    pe.wait_ge(xn2lo_ready, b + 1)
                if n == 0:
                    pe.wait_ge(wlo_ready, CONV1 + 1)
                if n < 2:
                    pe.wait_ge(qsq_ready, CH * B)
                else:
                    pe.wait_ge(gelu_ready, n - 1)
                for c in range(CH):
                    cols = slice(j * P, (j + 1) * P)
                    mm = split_mm(ps[:, CONV1_BANK + n % 2, :], c1_hi[:, c, cols], c1_lo[:, c, cols],
                                  xn_hi[:, b, c, :], xn_lo[:, b, c, :], c == 0, c == CH - 1)
                mm.then_inc(c1_done, 1)

            def conv2(b, o):
                if b == 0:
                    pe.wait_ge(wlo_ready, CONV2 + 1)
                    pe.wait_ge(x1_ready, CH * (B - 1) + o + 1)
                else:
                    pe.wait_ge(h1_ready, CH * (b - 1) + o + 1)
                for j in range(HT):
                    if o == 0:
                        pe.wait_ge(gelo_ready, HT * b + j + 1)
                    cols = slice(o * P, (o + 1) * P)
                    mm = split_mm(ps[:, CONV2_BANK + o, :], c2_hi[:, j, cols], c2_lo[:, j, cols],
                                  ghi[:, b % 2, j, :], glo[:, b % 2, j, :], j == 0, j == HT - 1)
                mm.then_inc(c2_done, 1)

            def ffn(b):
                pe.wait_ge(nlo_ready, b + 1)
                if b == 0:
                    pe.wait_ge(mlo_ready, 1)
                for o in range(CH):
                    if b == 0 and o == 0:
                        pe.wait_ge(xn2_ready, B)
                    elif b == 0:
                        pe.wait_ge(glo_ready, B)
                    else:
                        pe.wait_ge(ffn_taken, CH * (b - 1) + o + 1)
                    for c in range(CH):
                        cols = slice(o * P, (o + 1) * P)
                        mm = split_mm(ps[:, FFN_BANKS[o], :], m_hi[:, c, cols], m_lo[:, c, cols],
                                      xn_hi[:, b, c, :], xn_lo[:, b, c, :], c == 0, c == CH - 1)
                    mm.then_inc(ffn_done, 1)

            def mean1(b):
                pe.wait_ge(hsum1_ready, b + 1)
                if b >= 1:
                    pe.wait_ge(hc1_ready, b)
                nc.tensor.matmul(ps[:, MEAN1_BANK, :], mean_w[:], hsum[:], start=True, stop=True).then_inc(mean1_done, 1)

            def ss1(b):
                if b >= 1:
                    pe.wait_ge(st1_ready, b)
                square_sums(b, sq, sqsum1_ready, SS1_COL, ss1_done)

            def ss2(b):
                if b + 2 <= B:
                    pe.wait_ge(den_ready, b + 2)
                if b == B - 1:
                    pe.wait_ge(st2_ready, b)
                square_sums(b, sq2, sqsum2_ready, SS2_COL, ss2_done)

            def mean3(b):
                pe.wait_ge(hsum3_ready, b + 1)
                if b == 0:
                    pe.wait_ge(v_ready, TT * B)
                elif b == 1:
                    pe.wait_ge(scaled, 1)
                elif b == 2:
                    pe.wait_ge(gelu_ready, HT * B - 1)
                else:
                    pe.wait_ge(hc3_ready, b)
                nc.tensor.matmul(ps[:, MEAN2_BANKS[b], :], mean_w[:], hsum[:], start=True, stop=True).then_inc(mean3_done, 1)

            def ss3(b):
                if b == 0:
                    pe.wait_ge(st2_ready, B)
                else:
                    pe.wait_ge(st3_ready, b)
                square_sums(b, sq, sqsum3_ready, SS3_COL, ss3_done)

            pe.wait_ge(consts_ready, 5)
            for b in range(B):
                tok_mix(b, 0)
                if b >= 1:
                    mean1(b - 1)
                tok_mix(b, 1)
                tok_mix(b, 2)
                if b >= 1:
                    ss1(b - 1)
                tok_mix(b, 3)
                if b >= 1:
                    bc1(b - 1)
            dft_uv(0)
            mean1(3)
            dft_uv(1)
            qkv(0, 0)
            ss1(3)
            qkv(0, 1)
            dft_m()
            bc1(3)
            for j in range(2, TT + CH):
                qkv(0, j)
            for b in range(1, B):
                qkv(b, 0)
                qkv(b, 1)
                kv(b - 1)
                if b == 3:
                    ss2(0)
                qkv(b, 2)
                kv_turn(b - 1)
                denominators(b - 1)
                if b >= 2:
                    attention(b - 2)
                qkv(b, 3)
                kv_proj(b - 1)
                z_channels(b - 1)
                if b == 3:
                    bc2(0)
                qkv(b, 4)
                if b == 3:
                    ss2(1)
                qkv(b, 5)
            kv(3)
            attention(2)
            kv_turn(3)
            bc2(1)
            conv1(0, 0)
            denominators(3)
            conv1(0, 1)
            kv_proj(3)
            ss2(2)
            conv1(0, 2)
            z_channels(3)
            conv1(0, 3)
            conv1(1, 0)
            bc2(2)
            conv1(1, 1)
            attention(3)
            conv1(1, 2)
            conv1(1, 3)
            conv2(0, 0)
            conv2(0, 1)
            ss2(3)
            conv1(2, 0)
            bc2(3)
            conv1(2, 1)
            conv1(2, 2)
            mean3(0)
            conv1(2, 3)
            conv2(1, 0)
            conv2(1, 1)
            ss3(0)
            conv1(3, 0)
            conv1(3, 1)
            bc3(0)
            ffn(0)
            conv1(3, 2)
            conv1(3, 3)
            mean3(1)
            conv2(2, 0)
            conv2(2, 1)
            ss3(1)
            conv2(3, 0)
            mean3(2)
            bc3(1)
            conv2(3, 1)
            ffn(1)
            ss3(2)
            mean3(3)
            ffn(2)
            bc3(2)
            ss3(3)
            ffn(3)
            bc3(3)

        @block.scalar
        def _(act):
            def copy(dst, src, done):
                nc.scalar.activation(dst, src, ACT.Copy).then_inc(done, 1)

            def wtok_split(d):
                act.wait_ge(wtok_ready, d + 1)
                copy(wtok_hi[:, d, :], wtok[:, d, :], wtok_hi_ready)

            def x_split(b, d):
                act.wait_ge(x_in[d], 16 * (b + 1))
                if b >= 1:
                    act.wait_ge(tok_chunk, D * (b - 1) + d + 1)
                copy(xhi_ring[:, d, :], x_ring[:, d, :], xhi_ready)

            def h_out(b):
                for o in range(CH):
                    if o == 0:
                        act.wait_ge(tok_half0, b + 1)
                    else:
                        act.wait_ge(tok_chunk, D * (b + 1))
                    copy(h[:, o, b * T:(b + 1) * T], ps[:, TOK_BANK + o, :], h_ready)

            def square1(b):
                act.wait_ge(hc1_ready, b + 1)
                if b >= 1:
                    act.wait_ge(ss1_done, b)
                nc.scalar.activation(sq[:], hc[:], ACT.Square).then_inc(sq1_ready, 1)

            def xn_split(b):
                act.wait_ge(xn_ready, b + 1)
                copy(xn_hi[:, b], hc[:], xnhi_ready)

            def weight_split(n, dst, src):
                act.wait_ge(wscaled, n + 1)
                copy(dst, src, whi_ready)

            def k_square(b, t):
                act.wait_ge(qkv_done, (TT + CH) * b + t + 1)
                if b >= 2:
                    act.wait_ge(kv_done, b - 1)
                if b == 0 and t == 0:
                    act.wait_ge(m_done, 1)
                nc.scalar.activation(k[:, b % 2, t, :], ps[:, QKV_BANKS[((TT + CH) * b + t) % 4], 0:C],
                                     ACT.Square).then_inc(ksq_ready, 1)

            def k_exp(b):
                act.wait_ge(ksq_ready, TT * (b + 1))
                nc.scalar.activation(k[:, b % 2], k[:, b % 2], ACT.Exp, scale=-0.5).then_inc(k_ready, 1)

            def q_square(b, o):
                act.wait_ge(qkv_done, (TT + CH) * b + TT + o + 1)
                if b >= 2:
                    act.wait_ge(qzlo_ready, b - 1)
                elif b == 0 and o == 0:
                    act.wait_ge(wlo_ready, CONV2 + 1)
                nc.scalar.activation(q[:, b % 2, o, :], ps[:, QKV_BANKS[((TT + CH) * b + TT + o) % 4], :],
                                     ACT.Square).then_inc(qsq_ready, 1)

            def q_exp(b):
                act.wait_ge(qsq_ready, CH * (b + 1))
                nc.scalar.activation(q[:, b % 2], q[:, b % 2], ACT.Exp, scale=-0.5).then_inc(q_ready, 1)

            def z_expand(b):
                act.wait_ge(z_ready, b + 1)
                if b >= 1:
                    act.wait_ge(zt_done, b)
                copy(zx.rearrange("p (h d) -> p h d", d=DH),
                     z[:].unsqueeze(2).to_broadcast([P, TT * CH * HPH, DH]), zx_ready)

            def g_split(b):
                act.wait_ge(g_done, b + 1)
                if b >= 1:
                    act.wait_ge(attn_done, CH * b)
                copy(g_hi[:].rearrange("p c n -> p (c n)"), ps[:, KV_BANK, :], ghi_ready)

            def qz_split(b):
                act.wait_ge(qz_ready, b + 1)
                if b >= 2:
                    act.wait_ge(attn_done, CH * (b - 1))
                copy(qz_hi[:, b % 2], q[:, b % 2], qzhi_ready)

            def square2(b):
                act.wait_ge(x1_ready, CH * (b + 1))
                if b >= 1:
                    act.wait_ge(ss2_done, b)
                nc.scalar.activation(sq2, tok(u, b), ACT.Square).then_inc(sq2_ready, 1)

            def xn2_split(b):
                act.wait_ge(xn2_ready, b + 1)
                copy(xn_hi[:, b], xn2, xn2hi_ready)

            def gelu(b, j):
                act.wait_ge(c1_done, HT * b + j + 1)
                if b >= 1:
                    act.wait_ge(gelo_ready, HT * (b - 1) + j + 1)
                nc.scalar.activation(g[:, j, :], ps[:, CONV1_BANK + (HT * b + j) % 2, :], ACT.Gelu,
                                     bias=vecs[:, V_CONV1B + j:V_CONV1B + j + 1]).then_inc(gelu_ready, 1)

            def gelu_hi(b, j):
                act.wait_ge(gelu_ready, HT * b + j + 1)
                if b >= 2:
                    act.wait_ge(c2_done, CH * (b - 1))
                copy(ghi[:, b % 2, j, :], g[:, j, :], gehi_ready)

            def square3(b):
                act.wait_ge(hc3_ready, b + 1)
                if b >= 1:
                    act.wait_ge(ss3_done, b)
                nc.scalar.activation(sq[:], hc[:], ACT.Square).then_inc(sq3_ready, 1)

            def h1_split(b):
                act.wait_ge(h1_ready, CH * (b + 1))
                copy(xn_hi[:, b], tok(h, b), nhi_ready)

            def ffn_out(b, o):
                act.wait_ge(ffn_done, CH * b + o + 1)
                if b == 0 and o == 0:
                    act.wait_ge(xn2lo_ready, B)
                elif b == 1 and o == 0:
                    act.wait_ge(ss2_done, B)
                elif b >= 2:
                    act.wait_ge(out_ready, CH * (b - 2) + o + 1)
                copy(fout[b % 2][:, o, :], ps[:, FFN_BANKS[o], :], ffn_taken)

            def m_split():
                act.wait_ge(m_done, 1)
                nc.scalar.activation(m_hi[:].rearrange("p c n -> p (c n)"), ps[:, DFT_M_BANK, :], ACT.Copy,
                                     scale=1.0 / C).then_inc(mhi_ready, 1)

            for d in range(D):
                wtok_split(d)
                x_split(0, d)
            for d in range(3):
                x_split(1, d)
            for b in range(B):
                h_out(b)
                if b + 1 < B:
                    x_split(b + 1, 3)
                if b >= 1:
                    xn_split(b - 1)
                square1(b)
                if b == 3:
                    weight_split(CONV2, c2_hi[:].rearrange("p c n -> p (c n)"), stage[:, 0:HT * C])
                if b + 2 < B:
                    x_split(b + 2, 0)
                if b + 2 < B:
                    x_split(b + 2, 1)
                if b == 0:
                    weight_split(QKV, qkv_hi[:].rearrange("p c n -> p (c n)"), stage[:, 0:CH * 3 * C])
                if b == 1:
                    weight_split(CONV1, c1_hi[:].rearrange("p c n -> p (c n)"), stage[:, 0:CH * HID])
                if b + 2 < B:
                    x_split(b + 2, 2)
            m_split()
            k_square(0, 0)
            k_square(0, 1)
            k_square(0, 2)
            k_square(0, 3)
            k_exp(0)
            xn_split(3)
            q_square(0, 0)
            q_square(0, 1)
            q_exp(0)
            for b in range(1, B):
                if b == 3:
                    square2(0)
                k_square(b, 0)
                k_square(b, 1)
                k_square(b, 2)
                z_expand(b - 1)
                k_square(b, 3)
                if b == 3:
                    square2(1)
                g_split(b - 1)
                k_exp(b)
                qz_split(b - 1)
                q_square(b, 0)
                q_square(b, 1)
                q_exp(b)

            def gelus(b, *tiles):
                for j in tiles:
                    gelu(b, j)
                    gelu_hi(b, j)

            xn2_split(0)
            square2(2)
            gelus(0, 0)
            z_expand(3)
            gelus(0, 1)
            xn2_split(1)
            g_split(3)
            gelus(0, 2)
            gelus(0, 3)
            qz_split(3)
            gelus(1, 0)
            xn2_split(2)
            gelus(1, 1)
            square2(3)
            gelus(1, 2, 3)
            gelus(2, 0)
            xn2_split(3)
            gelus(2, 1)
            h1_split(0)
            gelus(2, 2)
            square3(0)
            gelus(2, 3)
            gelus(3, 0)
            h1_split(1)
            gelus(3, 1)
            ffn_out(0, 0)
            ffn_out(0, 1)
            gelus(3, 2, 3)
            square3(1)
            h1_split(2)
            square3(2)
            h1_split(3)
            ffn_out(1, 0)
            ffn_out(1, 1)
            square3(3)
            for b in (2, 3):
                for o in range(CH):
                    ffn_out(b, o)

        @block.gpsimd
        def _(pool):
            def constants():
                nc.gpsimd.memset(ones[:], 1.0).then_inc(consts_ready, 1)
                nc.gpsimd.memset(mean_w[:], 1.0 / C).then_inc(consts_ready, 1)
                nc.gpsimd.memset(minus_half[:], -0.5).then_inc(consts_ready, 1)
                nc.gpsimd.memset(ident[:], 0.0).then_inc(id_zeroed, 1)
                nc.gpsimd.memset(headmask[:], 1.0).then_inc(mask_step, 1)
                pool.wait_ge(id_zeroed, 1)
                nc.gpsimd.affine_select(out=ident[:], in_=ident[:], compare_op=ALU.not_equal, fill=1.0, base=0,
                                        pattern=[[-1, P]], channel_multiplier=1).then_inc(consts_ready, 1)
                m3 = headmask[:].rearrange("p (a d) -> p a d", d=DH)
                pool.wait_ge(mask_step, 1)
                nc.gpsimd.affine_select(out=m3, in_=m3, compare_op=ALU.is_ge, fill=0.0, base=0,
                                        pattern=[[-DH, HPH], [0, DH]], channel_multiplier=1).then_inc(mask_step, 1)
                pool.wait_ge(mask_step, 2)
                nc.gpsimd.affine_select(out=m3, in_=m3, compare_op=ALU.is_ge, fill=0.0, base=DH - 1,
                                        pattern=[[DH, HPH], [0, DH]], channel_multiplier=-1).then_inc(consts_ready, 1)

            def wtok_lo_split(d):
                pool.wait_ge(wtok_hi_ready, d + 1)
                nc.gpsimd.tensor_tensor(wtok_lo[:, d, :], wtok[:, d, :], wtok_hi[:, d, :].bitcast(F32),
                                        ALU.subtract).then_inc(wtok_lo_ready, 1)

            def gains():
                pool.wait_ge(vec_in, 16)
                nc.gpsimd.tensor_scalar(gain[:], vecs[:, V_SCALE1:V_SCALE1 + 4], RMS_GAIN, 1.0, ALU.mult,
                                        ALU.mult).then_inc(gains_ready, 1)
                for n, col in enumerate((V_PROJB, V_CONV2B)):
                    nc.gpsimd.tensor_tensor(gbias[:, 2 * n:2 * n + 2], vecs[:, col:col + 2],
                                            vecs[:, V_GAMMA:V_GAMMA + 2], ALU.mult).then_inc(gains_ready, 1)

            def scale_weights(n, width, loaded):
                pool.wait_ge(loaded, 16)
                for c in range(CH):
                    rows = stage[:, c * width:(c + 1) * width]
                    last = nc.gpsimd.tensor_scalar(rows, rows, gain[:, 2 * n + c:2 * n + c + 1], 1.0, ALU.mult,
                                                   ALU.mult)
                    if c == 0:
                        last.then_inc(mask_step, 1)
                last.then_inc(wscaled, 1)

            def weight_lo(n, dst, hi, src):
                pool.wait_ge(whi_ready, n + 1)
                nc.gpsimd.tensor_tensor(dst, src, hi.bitcast(F32), ALU.subtract).then_inc(wlo_ready, 1)

            def rn1_pow(b):
                for n in range(2):
                    pool.wait_ge(st1_ready, b + 1)
                    if b >= 1:
                        pool.wait_ge(bc1_done, 2 * (b - 1) + n + 1)
                    cols = slice(n * TT, (n + 1) * TT)
                    nc.gpsimd.tensor_tensor(rn1[:, cols], st1[:, cols], minus_half[:, cols],
                                            ALU.pow).then_inc(rn1_ready, 1)

            def u_bias(b):
                pool.wait_ge(u_ready, b + 1)
                for c in range(CH):
                    a = u[:, c, b * T:(b + 1) * T]
                    nc.gpsimd.tensor_scalar(a, a, gbias[:, c:c + 1], 1.0, ALU.add, ALU.mult).then_inc(ub_ready, 1)

            def xn_lo_split(b):
                pool.wait_ge(xnhi_ready, b + 1)
                nc.gpsimd.tensor_tensor(xn_lo[:, b], hc[:], xn_hi[:, b].bitcast(F32),
                                        ALU.subtract).then_inc(xnlo_ready, 1)

            def rn_pow(b, st, ready, rn, used, done):
                pool.wait_ge(ready, b + 1)
                if b >= 1:
                    pool.wait_ge(used, b)
                nc.gpsimd.tensor_tensor(rn[:], st[:], minus_half[:, 0:TT], ALU.pow).then_inc(done, 1)

            def square_sum(b, squares, ready, done):
                pool.wait_ge(ready, b + 1)
                nc.gpsimd.tensor_tensor(squares[:, 0, :], squares[:, 0, :], squares[:, 1, :], ALU.add).then_inc(done, 1)

            def rn2_pow(b):
                rn_pow(b, st2, st2_ready, rn2, bc2_done, rn2_ready)

            def rn3_pow(b):
                rn_pow(b, st3, st3_ready, rn3, bc3_done, rn3_ready)

            constants()
            for d in range(D):
                wtok_lo_split(d)
            gains()
            pool.wait_ge(gains_ready, 3)
            scale_weights(0, 3 * C, qkv_in)
            for b in range(B):
                square_sum(b, sq, sq1_ready, sqsum1_ready)
                rn1_pow(b)
                if b == 0:
                    weight_lo(QKV, qkv_lo[:].rearrange("p c n -> p (c n)"), qkv_hi[:].rearrange("p c n -> p (c n)"),
                              stage[:, 0:CH * 3 * C])
                    scale_weights(1, HID, c1_in)
                if b == 1:
                    weight_lo(CONV1, c1_lo[:].rearrange("p c n -> p (c n)"), c1_hi[:].rearrange("p c n -> p (c n)"),
                              stage[:, 0:CH * HID])
                    pool.wait_ge(c2_in, 16)
                    nc.gpsimd.nop().then_inc(wscaled, 1)
                if b == 3:
                    weight_lo(CONV2, c2_lo[:].rearrange("p c n -> p (c n)"), c2_hi[:].rearrange("p c n -> p (c n)"),
                              stage[:, 0:HT * C])
                if b >= 1:
                    u_bias(b - 1)
            pool.wait_ge(m_done, 1)
            for r in range(2):
                nc.gpsimd.memset(v[:, r, :, :, P:P + 1], 1.0).then_inc(v_ones, 1)
            xn_lo_split(3)
            u_bias(3)
            for b in range(B):
                square_sum(b, sq2, sq2_ready, sqsum2_ready)
                rn2_pow(b)
            for b in range(B):
                square_sum(b, sq, sq3_ready, sqsum3_ready)
                rn3_pow(b)

        @block.vector
        def _(dve):
            def wtok_build(d):
                if d == 1:
                    dve.wait_ge(w_rest_in, 16)
                for c in range(CH):
                    last = nc.vector.tensor_tensor(wtok[:, d, c * C:(c + 1) * C], ws_sb[:, c * C:(c + 1) * C],
                                                   w_bc[:, d, :], ALU.mult)
                last.then_inc(wtok_ready, 1)

            def x_lo_split(b, d):
                dve.wait_ge(xhi_ready, D * b + d + 1)
                nc.vector.tensor_tensor(xlo_ring[:, d, :], x_ring[:, d, :], xhi_ring[:, d, :].bitcast(F32),
                                        ALU.subtract).then_inc(xlo_ready, 1)

            def hsum1(b):
                dve.wait_ge(h_ready, CH * (b + 1))
                if b >= 1:
                    dve.wait_ge(mean1_done, b)
                nc.vector.tensor_tensor(hsum[:], h[:, 0, b * T:(b + 1) * T], h[:, 1, b * T:(b + 1) * T],
                                        ALU.add).then_inc(hsum1_ready, 1)

            def mean_bank(bank):
                return ps[:, bank:bank + 1, :].to_broadcast([P, CH, T])

            def center1(b):
                dve.wait_ge(mean1_done, b + 1)
                if b >= 1:
                    dve.wait_ge(xnlo_ready, b)
                nc.vector.tensor_tensor(hc[:], tok(h, b), mean_bank(MEAN1_BANK), ALU.subtract).then_inc(hc1_ready, 1)

            def stats1(b):
                dve.wait_ge(ss1_done, b + 1)
                if b >= 1:
                    dve.wait_ge(rn1_ready, 2 * b)
                nc.vector.tensor_copy(st1[:, 0:TT], ps[:, STAT_BANK, SS1_COL:SS1_COL + TT])
                nc.vector.tensor_scalar(st1[:, TT:2 * TT], ps[:, STAT_BANK, SS1_COL:SS1_COL + TT], 1.0 / C, LN_EPS,
                                        ALU.mult, ALU.add).then_inc(st1_ready, 1)

            def normalize1(b):
                dve.wait_ge(sq1_ready, b + 1)
                dve.wait_ge(bc1_done, 2 * b + 2)
                nc.vector.tensor_tensor(tok(u, b), hc[:], mean_bank(RSTD_BANK), ALU.mult).then_inc(u_ready, 1)
                dve.wait_ge(u_ready, b + 1)
                nc.vector.tensor_tensor(hc[:], hc[:], mean_bank(RNORM_BANK), ALU.mult).then_inc(xn_ready, 1)

            def xn_lo_split(b):
                dve.wait_ge(xnhi_ready, b + 1)
                nc.vector.tensor_tensor(xn_lo[:, b], hc[:], xn_hi[:, b].bitcast(F32),
                                        ALU.subtract).then_inc(xnlo_ready, 1)

            def neg_b():
                dve.wait_ge(dft_in, 32)
                nc.vector.tensor_scalar(neg_b_sb, freq_sb[:, 1], -1.0, None, ALU.mult).then_inc(negb_ready, 1)

            def uv_center(n):
                a = uv[:, n]
                dve.wait_ge(uv_done, n + 1)
                nc.vector.tensor_copy(a.rearrange("p c n -> p (c n)"), ps[:, DFT_U_BANK + n, :]).then_inc(uv_raw, 1)
                dve.wait_ge(uv_raw, n + 1)
                nc.vector.reduce_sum(row_sum[:, n], a, axis=mybir.AxisListType.X).then_inc(uv_sum, 1)
                dve.wait_ge(uv_sum, n + 1)
                nc.vector.tensor_scalar(row_mean[:, n], row_sum[:, n], 1.0 / C, None, ALU.mult).then_inc(uv_mean, 1)
                dve.wait_ge(uv_mean, n + 1)
                nc.vector.tensor_tensor(a, a, row_mean[:, n].unsqueeze(2).to_broadcast([P, CH, C]),
                                        ALU.subtract).then_inc(uv_ready, 1)

            def m_lo_split():
                dve.wait_ge(mhi_ready, 1)
                nc.vector.scalar_tensor_tensor(out=m_lo[:].rearrange("p c n -> p (c n)"), in0=ps[:, DFT_M_BANK, :],
                                               scalar=1.0 / C, in1=m_hi[:].rearrange("p c n -> p (c n)").bitcast(F32),
                                               op0=ALU.mult, op1=ALU.subtract).then_inc(mlo_ready, 1)

            def v_copy(b, t):
                dve.wait_ge(ksq_ready, TT * b + t + 1)
                if b >= 2:
                    dve.wait_ge(kv_done, b - 1)
                bank = QKV_BANKS[((TT + CH) * b + t) % 4]
                nc.vector.tensor_copy(v[:, b % 2, t, :, 0:P],
                                      ps[:, bank, C:2 * C].rearrange("p (c n) -> p c n", c=CH)).then_inc(v_ready, 1)

            def kv_mask(b):
                dve.wait_ge(kv_done, b + 1)
                if b >= 1:
                    dve.wait_ge(kvt_done, b)
                    dve.wait_ge(den_done, b)
                else:
                    dve.wait_ge(consts_ready, 5)
                kv_ps = ps[:, KV_BANK, 0:CH * (P + 1)].rearrange("p (c n) -> p c n", c=CH)
                nc.vector.tensor_tensor(kv_masked[:], kv_ps[:, :, 0:P], headmask[:].unsqueeze(1).to_broadcast([P, CH, P]),
                                        ALU.mult)
                for c in range(CH):
                    last = nc.vector.tensor_scalar(ksum_masked[:, c, :], headmask[:, 0:P:DH], kv_ps[:, c, P:P + 1],
                                                   None, ALU.mult)
                last.then_inc(kvm_ready, 1)

            def kvt_out(b):
                dve.wait_ge(kvt_done, b + 1)
                if b >= 1:
                    dve.wait_ge(g_done, b)
                nc.vector.tensor_copy(kvt[:].rearrange("p c n -> p (c n)"), ps[:, KV_BANK, 0:C]).then_inc(kvt_ready, 1)

            def reciprocals(b):
                dve.wait_ge(den_done, b + 1)
                nc.vector.tensor_scalar(den[:], ps[:, STAT_BANK, DEN_COL:DEN_COL + TT * CH * HPH], DEN_EPS, None,
                                        ALU.add).then_inc(den_ready, 1)
                dve.wait_ge(den_ready, b + 1)
                if b >= 1:
                    dve.wait_ge(zx_ready, b)
                nc.vector.reciprocal(z[:], den[:]).then_inc(z_ready, 1)

            def scale_q(b):
                dve.wait_ge(zt_done, b + 1)
                nc.vector.tensor_tensor(q[:, b % 2], q[:, b % 2], ps[:, Z_BANK:Z_BANK + CH, :],
                                        ALU.mult).then_inc(qz_ready, 1)

            def qz_lo_split(b):
                dve.wait_ge(qzhi_ready, b + 1)
                nc.vector.tensor_tensor(qz_lo[:, b % 2], q[:, b % 2], qz_hi[:, b % 2].bitcast(F32),
                                        ALU.subtract).then_inc(qzlo_ready, 1)

            def g_lo_split(b):
                dve.wait_ge(ghi_ready, b + 1)
                nc.vector.tensor_tensor(g_lo[:].rearrange("p c n -> p (c n)"), ps[:, KV_BANK, :],
                                        g_hi[:].rearrange("p c n -> p (c n)").bitcast(F32),
                                        ALU.subtract).then_inc(glo_ready, 1)

            def x1(b):
                for o in range(CH):
                    dve.wait_ge(attn_done, CH * b + o + 1)
                    dve.wait_ge(ub_ready, CH * b + o + 1)
                    a = u[:, o, b * T:(b + 1) * T]
                    nc.vector.scalar_tensor_tensor(out=a, in0=ps[:, Z_BANK + o, :],
                                                   scalar=vecs[:, V_GAMMA + o:V_GAMMA + o + 1], in1=a,
                                                   op0=ALU.mult, op1=ALU.add).then_inc(x1_ready, 1)

            def stats2(b):
                dve.wait_ge(ss2_done, b + 1)
                if b >= 1:
                    dve.wait_ge(rn2_ready, b)
                nc.vector.tensor_copy(st2[:], ps[:, STAT_BANK, SS2_COL:SS2_COL + TT]).then_inc(st2_ready, 1)

            def normalize2(b):
                dve.wait_ge(bc2_done, b + 1)
                if b >= 1:
                    dve.wait_ge(xn2lo_ready, b)
                nc.vector.tensor_tensor(xn2, tok(u, b), mean_bank(RMS_BANK), ALU.mult).then_inc(xn2_ready, 1)

            def xn2_lo_split(b):
                dve.wait_ge(xn2hi_ready, b + 1)
                nc.vector.tensor_tensor(xn_lo[:, b], xn2, xn_hi[:, b].bitcast(F32), ALU.subtract).then_inc(xn2lo_ready, 1)

            def h_plus_x1(b):
                dve.wait_ge(x1_ready, CH * (b + 1))
                for o in range(CH):
                    cols = slice(b * T, (b + 1) * T)
                    nc.vector.scalar_tensor_tensor(out=h[:, o, cols], in0=u[:, o, cols], scalar=gbias[:, 2 + o:3 + o],
                                                   in1=h[:, o, cols], op0=ALU.add, op1=ALU.add).then_inc(hx_ready, 1)

            def gelu_split(b, j):
                dve.wait_ge(gehi_ready, HT * b + j + 1)
                nc.vector.tensor_tensor(glo[:, b % 2, j, :], g[:, j, :], ghi[:, b % 2, j, :].bitcast(F32),
                                        ALU.subtract).then_inc(gelo_ready, 1)

            def h1(b):
                for o in range(CH):
                    dve.wait_ge(c2_done, CH * b + o + 1)
                    dve.wait_ge(hx_ready, CH * b + o + 1)
                    a = h[:, o, b * T:(b + 1) * T]
                    nc.vector.scalar_tensor_tensor(out=a, in0=ps[:, CONV2_BANK + o, :],
                                                   scalar=vecs[:, V_GAMMA + o:V_GAMMA + o + 1], in1=a,
                                                   op0=ALU.mult, op1=ALU.add).then_inc(h1_ready, 1)

            def hsum3(b):
                dve.wait_ge(h1_ready, CH * (b + 1))
                if b >= 1:
                    dve.wait_ge(mean3_done, b)
                nc.vector.tensor_tensor(hsum[:], h[:, 0, b * T:(b + 1) * T], h[:, 1, b * T:(b + 1) * T],
                                        ALU.add).then_inc(hsum3_ready, 1)

            def center3(b):
                dve.wait_ge(mean3_done, b + 1)
                if b >= 1:
                    dve.wait_ge(sq3_ready, b)
                nc.vector.tensor_tensor(hc[:], tok(h, b), mean_bank(MEAN2_BANKS[b]), ALU.subtract).then_inc(hc3_ready, 1)

            def stats3(b):
                dve.wait_ge(ss3_done, b + 1)
                if b >= 1:
                    dve.wait_ge(rn3_ready, b)
                nc.vector.tensor_scalar(st3[:], ps[:, STAT_BANK, SS3_COL:SS3_COL + TT], 1.0 / C, LN_EPS,
                                        ALU.mult, ALU.add).then_inc(st3_ready, 1)

            def h1_lo_split(b):
                dve.wait_ge(nhi_ready, b + 1)
                nc.vector.tensor_tensor(xn_lo[:, b], tok(h, b), xn_hi[:, b].bitcast(F32),
                                        ALU.subtract).then_inc(nlo_ready, 1)

            def result(b):
                a = fout[b % 2]
                dve.wait_ge(ffn_taken, CH * (b + 1))
                dve.wait_ge(bc3_done, b + 1)
                dve.wait_ge(nlo_ready, b + 1)
                nc.vector.tensor_tensor(a, a, mean_bank(RSTD2_BANK), ALU.mult).then_inc(scaled, 1)
                dve.wait_ge(scaled, b + 1)
                for o in range(CH):
                    ho = h[:, o, b * T:(b + 1) * T]
                    nc.vector.scalar_tensor_tensor(out=ho, in0=a[:, o, :], scalar=vecs[:, V_FFNB + o:V_FFNB + o + 1],
                                                   in1=ho, op0=ALU.add, op1=ALU.add).then_inc(out_ready, 1)

            dve.wait_ge(ws_in, 16)
            dve.wait_ge(w_in, 16)
            wtok_build(0)
            wtok_build(1)
            for d in range(D):
                x_lo_split(0, d)
                if d + 2 < D:
                    wtok_build(d + 2)
            for d in range(3):
                x_lo_split(1, d)
            for b in range(B):
                hsum1(b)
                if b >= 1:
                    normalize1(b - 1)
                if b + 1 < B:
                    x_lo_split(b + 1, 3)
                if b >= 1:
                    xn_lo_split(b - 1)
                center1(b)
                if b + 2 < B:
                    x_lo_split(b + 2, 0)
                    x_lo_split(b + 2, 1)
                if b == 1:
                    neg_b()
                if b == 3:
                    uv_center(0)
                    uv_center(1)
                stats1(b)
                if b + 2 < B:
                    x_lo_split(b + 2, 2)
            v_copy(0, 0)
            v_copy(0, 1)
            m_lo_split()
            v_copy(0, 2)
            v_copy(0, 3)
            normalize1(3)
            for b in range(1, B):
                v_copy(b, 0)
                v_copy(b, 1)
                kv_mask(b - 1)
                if b == 3:
                    stats2(0)
                v_copy(b, 2)
                kvt_out(b - 1)
                reciprocals(b - 1)
                if b >= 2:
                    x1(b - 2)
                v_copy(b, 3)
                g_lo_split(b - 1)
                scale_q(b - 1)
                if b == 3:
                    normalize2(0)
                qz_lo_split(b - 1)
            stats2(1)
            kv_mask(3)
            xn2_lo_split(0)
            x1(2)
            kvt_out(3)
            normalize2(1)
            reciprocals(3)
            gelu_split(0, 0)
            xn2_lo_split(1)
            g_lo_split(3)
            gelu_split(0, 1)
            stats2(2)
            scale_q(3)
            gelu_split(0, 2)
            qz_lo_split(3)
            gelu_split(0, 3)
            normalize2(2)
            xn2_lo_split(2)
            gelu_split(1, 0)
            gelu_split(1, 1)
            x1(3)
            gelu_split(1, 2)
            gelu_split(1, 3)
            h_plus_x1(0)
            stats2(3)
            h1(0)
            hsum3(0)
            normalize2(3)
            gelu_split(2, 0)
            xn2_lo_split(3)
            gelu_split(2, 1)
            h1_lo_split(0)
            center3(0)
            gelu_split(2, 2)
            h_plus_x1(1)
            gelu_split(2, 3)
            h1(1)
            hsum3(1)
            stats3(0)
            gelu_split(3, 0)
            h1_lo_split(1)
            gelu_split(3, 1)
            h_plus_x1(2)
            result(0)
            gelu_split(3, 2)
            gelu_split(3, 3)
            center3(1)
            h_plus_x1(3)
            h1(2)
            hsum3(2)
            stats3(1)
            h1_lo_split(2)
            center3(2)
            h1(3)
            hsum3(3)
            stats3(2)
            h1_lo_split(3)
            center3(3)
            result(1)
            stats3(3)
            result(2)
            result(3)


def kernel(**inputs):
    import numpy as np
    import concourse.bacc as bacc
    from concourse.bass_utils import run_bass_kernel_spmd

    def halves(a):
        n = a.shape[0] // P
        return np.ascontiguousarray(a.reshape(n, P, -1).transpose(1, 0, 2).reshape(P, -1))

    get = {name: np.asarray(a) for name, a in inputs.items()}
    x = get["x"].reshape(B, T, CH, P, D).transpose(0, 4, 3, 2, 1)
    vectors = np.concatenate([get[n].reshape(-1, P).T for n in (
        "L0_attn_scale1", "L0_attn_scale2", "L0_attn_gamma", "L0_attn_proj_b", "L0_attn_conv2_b", "L0_ffn_bias",
        "L0_attn_conv1_b")], axis=1)
    angle = 2 * np.pi * (np.outer(np.arange(C), np.arange(C)) % C) / C
    arrays = {
        "x": np.ascontiguousarray(x.reshape(B, D, P, CH * T)),
        "ws": halves(get["L0_tok_weighted_sum"].T),
        "w": np.ascontiguousarray(np.broadcast_to(get["L0_tok_weight"].T.reshape(1, D * C), (P, D * C))),
        "vec": np.ascontiguousarray(vectors),
        "qkv_w": halves(get["L0_attn_qkv_w"].T),
        "proj_w": halves(get["L0_attn_proj_w"].T),
        "conv1_w": halves(get["L0_attn_conv1_w"].T),
        "conv2_w": halves(get["L0_attn_conv2_w"].T),
        "dft": np.concatenate([halves(np.cos(angle).astype(np.float32)), halves(np.sin(angle).astype(np.float32))], 1),
        "freq": np.concatenate([halves(get["L0_ffn_w_freq_real"]), halves(get["L0_ffn_w_freq_imag"])], 1),
    }
    nc = bacc.Bacc("TRN2", target_bir_lowering=False, num_devices=1)
    aps = {n: nc.dram_tensor(n, a.shape, F32, kind="ExternalInput").ap() for n, a in arrays.items()}
    out = nc.dram_tensor("out", (CH, P, B * T), F32, kind="ExternalOutput").ap()
    build(nc, out=out, **aps)
    result = run_bass_kernel_spmd(nc, [arrays], core_ids=[0])
    return np.ascontiguousarray(result.results[0]["out"].reshape(C, B, T).transpose(1, 2, 0))
```

```python
from contextlib import ExitStack

import concourse.bass as bass
from concourse import mybir

F32 = mybir.dt.float32
F32R = mybir.dt.float32r
ALU = mybir.AluOpType
ACT = mybir.ActivationFunctionType

P = 128
B = 4
T = 512
TT = T // P
C = 256
CH = C // P
D = 4
HID = 512
HT = HID // P
DH = 16
HPH = P // DH
LN_EPS = 1e-5
RMS_GAIN = C ** 0.5 + 1e-6
DEN_EPS = 1e-6
V_SCALE1, V_SCALE2, V_GAMMA, V_PROJB, V_CONV2B, V_FFNB, V_CONV1B = (CH * n for n in range(7))
V_END = V_CONV1B + HT
TOK_BANK = 0
MEAN1_BANK, STAT_BANK, RNORM_BANK, RSTD_BANK = 2, 3, 4, 5
DFT_U_BANK, DFT_V_BANK = 6, 7
QKV_BANKS = (0, 1, 6, 7)
KV_BANK = 2
Z_BANK = 4
RMS_BANK = 0
CONV1_BANK = 6
FFN_BANKS = ((0, 2), (0, 2), (4, 5), (7, 6))
CONV2_BANK = 4
MEAN2_BANKS = (1, 1, 6, 6)
RSTD2_BANK = 1
DFT_M_BANK = 2
WARM_UP = 13
DEN_COL, SS1_COL, SS2_COL, SS3_COL = 0, 64, 72, 80


def build(nc, x, ws, w, vec, qkv_w, proj_w, conv1_w, conv2_w, dft, freq, out):
    with ExitStack() as ctx:
        def sb(name, shape, dt=F32):
            return ctx.enter_context(nc.sbuf_tensor(name, shape, dt))

        def sem(name):
            return ctx.enter_context(nc.semaphore(name))

        x_ring = sb("x_ring", [P, D, CH * T])
        xhi_ring = sb("xhi_ring", [P, D, CH * T], F32R)
        xlo_ring = sb("xlo_ring", [P, D, CH * T], F32R)
        late = x_ring[:, :, :].rearrange("p a n -> p (a n)")
        g = late[:, 0:HT * T].rearrange("p (j n) -> p j n", j=HT)
        sq2 = late[:, HT * T:(HT + CH) * T].rearrange("p (c n) -> p c n", c=CH)
        xn2 = late[:, (HT + CH) * T:(HT + 2 * CH) * T].rearrange("p (c n) -> p c n", c=CH)
        ghi = xhi_ring[:, :, :].rearrange("p a n -> p (a n)").rearrange("p (r j n) -> p r j n", r=2, j=HT)
        glo = xlo_ring[:, :, :].rearrange("p a n -> p (a n)").rearrange("p (r j n) -> p r j n", r=2, j=HT)
        fout = (xn2, sq2)
        wtok = sb("wtok", [P, D, CH * C])
        wtok_hi = sb("wtok_hi", [P, D, CH * C], F32R)
        wtok_lo = sb("wtok_lo", [P, D, CH * C], F32R)
        stage = wtok[:, :, :].rearrange("p a n -> p (a n)")
        q = wtok[:, :, :].rearrange("p a n -> p (a n)").rearrange("p (r c n) -> p r c n", r=2, c=CH)
        qz_hi = wtok_hi[:, :, :].rearrange("p a n -> p (a n)").rearrange("p (r c n) -> p r c n", r=2, c=CH)
        qz_lo = wtok_lo[:, :, :].rearrange("p a n -> p (a n)").rearrange("p (r c n) -> p r c n", r=2, c=CH)
        k = sb("k", [P, 2, TT, C])
        v = sb("v", [P, 2, TT, CH, P + 1])
        dft_sb = k[:, 0].rearrange("p t n -> p (t n)")[:, 0:2 * C].rearrange("p (a c n) -> p a c n", a=2, c=CH)
        freq_sb = k[:, 1].rearrange("p t n -> p (t n)").rearrange("p (a c n) -> p a c n", a=2, c=CH)
        uv_parts = v[:, 0].rearrange("p t c n -> p (t c n)")[:, 0:2 * CH * C].rearrange(
            "p (a m c n) -> p a m c n", a=2, m=CH, c=CH)
        late_v = v[:, 1].rearrange("p t c n -> p (t c n)")
        w_bc = late_v[:, 0:D * C].rearrange("p (d o) -> p d o", d=D)
        uv = late_v[:, 0:2 * CH * C].rearrange("p (a c n) -> p a c n", a=2, c=CH)
        h = sb("h", [P, CH, B * T])
        u = sb("u", [P, CH, B * T])
        xn_hi = sb("xn_hi", [P, B, CH, T], F32R)
        xn_lo = sb("xn_lo", [P, B, CH, T], F32R)
        hsum = sb("hsum", [P, T])
        ws_sb = hsum
        m_full = hsum[:].rearrange("p (m n) -> p m n", m=CH)
        xn = sb("xn", [P, CH, T])
        hc = xn
        sq = sb("sq", [P, CH, T])
        zx = sq[:].rearrange("p c n -> p (c n)")
        qkv_hi = sb("qkv_hi", [P, CH, 3 * C], F32R)
        qkv_lo = sb("qkv_lo", [P, CH, 3 * C], F32R)
        proj = sb("proj", [P, CH, C])
        c1_hi = sb("c1_hi", [P, CH, HID], F32R)
        c1_lo = sb("c1_lo", [P, CH, HID], F32R)
        c2_hi = sb("c2_hi", [P, HT, C], F32R)
        c2_lo = sb("c2_lo", [P, HT, C], F32R)
        m_hi = sb("m_hi", [P, CH, C], F32R)
        m_lo = sb("m_lo", [P, CH, C], F32R)
        vecs = sb("vecs", [P, V_END])
        gain = sb("gain", [P, 4])
        gbias = sb("gbias", [P, 4])
        ident = sb("ident", [P, P])
        mean_w = sb("mean_w", [P, P])
        ones = sb("ones", [P, 1])
        headmask = sb("headmask", [P, P])
        kv_masked = sb("kv_masked", [P, CH, P])
        kvt = sb("kvt", [P, CH, P])
        neg_b = sb("neg_b", [P, T])
        neg_b_sb = neg_b[:].rearrange("p (c n) -> p c n", c=CH)
        m_parts = neg_b[:].rearrange("p (m c n) -> p m c n", m=CH, c=CH)
        row_sum = sb("row_sum", [P, 2, CH])
        row_mean = sb("row_mean", [P, 2, CH])
        ksum_masked = sb("ksum_masked", [P, CH, HPH])
        g_hi = sb("g_hi", [P, CH, C], F32R)
        g_lo = sb("g_lo", [P, CH, C], F32R)
        den = sb("den", [P, TT * CH * HPH])
        z = sb("z", [P, TT * CH * HPH])
        minus_half = sb("minus_half", [P, 2 * TT])
        st1 = sb("st1", [P, 2 * TT])
        rn1 = sb("rn1", [P, 2 * TT])
        st2 = sb("st2", [P, TT])
        rn2 = sb("rn2", [P, TT])
        st3 = sb("st3", [P, TT])
        rn3 = sb("rn3", [P, TT])
        ps = ctx.enter_context(nc.psum_tensor("ps", [P, 8, T], F32))

        def tok(t, b):
            return t[:, :, b * T:(b + 1) * T]

        first_hi_ready, first_lo_ready = sem("first_hi_ready"), sem("first_lo_ready")
        x_in = [sem(f"x_in{s}") for s in range(D)]
        w_rest_in = sem("w_rest_in")
        ws_in, w_in, vec_in, qkv_in, proj_in, c1_in, c2_in, dft_in = (
            sem(n) for n in ("ws_in", "w_in", "vec_in", "qkv_in", "proj_in", "c1_in", "c2_in", "dft_in"))
        out_sent = sem("out_sent")
        v_ones, kvt_done, kvt_ready, sqsum1_ready, sqsum2_ready, sqsum3_ready, ffn_taken, scaled = (
            sem(n) for n in ("v_ones", "kvt_done", "kvt_ready", "sqsum1_ready", "sqsum2_ready", "sqsum3_ready",
                             "ffn_taken", "scaled"))
        consts_ready, id_zeroed, mask_step, gains_ready = (
            sem(n) for n in ("consts_ready", "id_zeroed", "mask_step", "gains_ready"))
        wtok_ready, wtok_hi_ready, wtok_lo_ready = sem("wtok_ready"), sem("wtok_hi_ready"), sem("wtok_lo_ready")
        xhi_ready, xlo_ready, tok_half0, tok_chunk, h_ready = (
            sem(n) for n in ("xhi_ready", "xlo_ready", "tok_half0", "tok_chunk", "h_ready"))
        wscaled, whi_ready, wlo_ready = sem("wscaled"), sem("whi_ready"), sem("wlo_ready")
        negb_ready, uv_done, uv_raw, uv_sum, uv_mean, uv_centered, uv_ready, m_done, m_raw, m_ready, mhi_ready, mlo_ready = (
            sem(n) for n in ("negb_ready", "uv_done", "uv_raw", "uv_sum", "uv_mean", "uv_centered", "uv_ready", "m_done",
                             "m_raw", "m_ready", "mhi_ready", "mlo_ready"))
        hsum1_ready, mean1_done, hc1_ready, sq1_ready, ss1_done, st1_ready, rn1_ready, bc1_done = (
            sem(n) for n in ("hsum1_ready", "mean1_done", "hc1_ready", "sq1_ready", "ss1_done", "st1_ready",
                             "rn1_ready", "bc1_done"))
        u_ready, xn_ready, ub_ready, xnhi_ready, xnlo_ready = (
            sem(n) for n in ("u_ready", "xn_ready", "ub_ready", "xnhi_ready", "xnlo_ready"))
        qkv_done, ksq_ready, qsq_ready, k_ready, q_ready, v_ready = (
            sem(n) for n in ("qkv_done", "ksq_ready", "qsq_ready", "k_ready", "q_ready", "v_ready"))
        kv_done, kvm_ready, den_done, den_ready, z_ready, zx_ready, zt_done = (
            sem(n) for n in ("kv_done", "kvm_ready", "den_done", "den_ready", "z_ready", "zx_ready", "zt_done"))
        g_done, ghi_ready, glo_ready, qz_ready, qzhi_ready, qzlo_ready, attn_done, x1_ready = (
            sem(n) for n in ("g_done", "ghi_ready", "glo_ready", "qz_ready", "qzhi_ready", "qzlo_ready",
                             "attn_done", "x1_ready"))
        sq2_ready, ss2_done, st2_ready, rn2_ready, bc2_done, xn2_ready, xn2hi_ready, xn2lo_ready, hx_ready = (
            sem(n) for n in ("sq2_ready", "ss2_done", "st2_ready", "rn2_ready", "bc2_done", "xn2_ready",
                             "xn2hi_ready", "xn2lo_ready", "hx_ready"))
        c1_done, gelu_ready, gehi_ready, gelo_ready, c2_done, h1_ready = (
            sem(n) for n in ("c1_done", "gelu_ready", "gehi_ready", "gelo_ready", "c2_done", "h1_ready"))
        hsum3_ready, mean3_done, hc3_ready, sq3_ready, ss3_done, st3_ready, rn3_ready, bc3_done = (
            sem(n) for n in ("hsum3_ready", "mean3_done", "hc3_ready", "sq3_ready", "ss3_done", "st3_ready",
                             "rn3_ready", "bc3_done"))
        nhi_ready, nlo_ready, ffn_done, out_ready = (
            sem(n) for n in ("nhi_ready", "nlo_ready", "ffn_done", "out_ready"))

        QKV, CONV1, CONV2 = range(3)

        block = ctx.enter_context(nc.Block())

        @block.sync
        def _(sp):
            def load_x(b, d):
                if b >= 1:
                    sp.wait_ge(xlo_ready, D * (b - 1) + d + 1)
                sp.dma_start(x_ring[:, d, :], x[b, d]).then_inc(x_in[d], 16)

            sp.dma_start(ws_sb[:], ws).then_inc(ws_in, 16)
            sp.dma_start(w_bc[:, 0:1, :].rearrange("p d o -> p (d o)"), w[:, 0:C]).then_inc(w_in, 16)
            load_x(0, 0)
            sp.dma_start(w_bc[:, 1:D, :].rearrange("p d o -> p (d o)"), w[:, C:D * C]).then_inc(w_rest_in, 16)
            for d in range(1, D):
                load_x(0, d)
            sp.dma_start(vecs[:], vec).then_inc(vec_in, 16)
            for d in range(D):
                load_x(1, d)
            sp.wait_ge(wtok_lo_ready, D)
            sp.dma_start(stage[:, 0:CH * 3 * C], qkv_w).then_inc(qkv_in, 16)
            sp.dma_start(dft_sb.rearrange("p a c n -> p (a c n)"), dft).then_inc(dft_in, 16)
            sp.dma_start(freq_sb.rearrange("p a c n -> p (a c n)"), freq).then_inc(dft_in, 16)
            sp.dma_start(proj[:].rearrange("p c n -> p (c n)"), proj_w).then_inc(proj_in, 16)
            for d in range(D):
                load_x(2, d)
            sp.wait_ge(wlo_ready, QKV + 1)
            sp.dma_start(stage[:, 0:CH * HID], conv1_w).then_inc(c1_in, 16)
            for d in range(D):
                load_x(3, d)
            sp.wait_ge(wlo_ready, CONV1 + 1)
            sp.dma_start(stage[:, 0:HT * C], conv2_w).then_inc(c2_in, 16)
            for b in range(B):
                for o in range(CH):
                    sp.wait_ge(out_ready, CH * b + o + 1)
                    sp.dma_start(out[o, :, b * T:(b + 1) * T], h[:, o, b * T:(b + 1) * T]).then_inc(out_sent, 16)
            sp.wait_ge(out_sent, 16 * CH * B)

        @block.tensor
        def _(pe):
            def split_mm(bank_ap, w_hi, w_lo, m_hi_, m_lo_, first, last):
                nc.tensor.matmul(bank_ap, w_hi, m_hi_, start=first, stop=False)
                nc.tensor.matmul(bank_ap, w_lo, m_hi_, start=False, stop=False)
                return nc.tensor.matmul(bank_ap, w_hi, m_lo_, start=False, stop=last)

            def tok_mix(b, d, halves=range(CH)):
                pe.wait_ge(xlo_ready, D * b + d + 1)
                for o in halves:
                    if d == 0:
                        pe.wait_ge(h_ready, CH * (b - 1) + o + 1)
                    for i in range(CH):
                        wc = slice(i * C + o * P, i * C + o * P + P)
                        mm = split_mm(ps[:, TOK_BANK + o, :], wtok_hi[:, d, wc], wtok_lo[:, d, wc],
                                      xhi_ring[:, d, i * T:(i + 1) * T], xlo_ring[:, d, i * T:(i + 1) * T],
                                      d == 0 and i == 0, d == D - 1 and i == CH - 1)
                    if d == D - 1 and o == 0:
                        mm.then_inc(tok_half0, 1)
                    elif o == CH - 1:
                        mm.then_inc(tok_chunk, 1)

            def square_sums(b, squares, ready, col, done):
                pe.wait_ge(ready, b + 1)
                for t in range(TT):
                    mm = nc.tensor.matmul(ps[:, STAT_BANK, col + t:col + t + 1], squares[:, 0, t * P:(t + 1) * P],
                                          ones[:, 0:1], start=True, stop=True)
                mm.then_inc(done, 1)

            def broadcast(bank, per_token):
                for t in range(TT):
                    mm = nc.tensor.transpose(ps[:, bank, t * P:(t + 1) * P],
                                             per_token[:, t:t + 1].to_broadcast([P, P]), ident[:])
                return mm

            def bc1(b):
                pe.wait_ge(rn1_ready, 2 * b + 1)
                if b >= 1:
                    pe.wait_ge(xn_ready, b)
                broadcast(RNORM_BANK, rn1[:, 0:TT]).then_inc(bc1_done, 1)
                pe.wait_ge(rn1_ready, 2 * b + 2)
                if b >= 1:
                    pe.wait_ge(u_ready, b)
                broadcast(RSTD_BANK, rn1[:, TT:2 * TT]).then_inc(bc1_done, 1)

            def bc2(b):
                pe.wait_ge(rn2_ready, b + 1)
                if b >= 1:
                    pe.wait_ge(xn2_ready, b)
                else:
                    pe.wait_ge(v_ready, TT * (B - 1) + 3)
                broadcast(RMS_BANK, rn2[:]).then_inc(bc2_done, 1)

            def bc3(b):
                pe.wait_ge(rn3_ready, b + 1)
                if b >= 2:
                    pe.wait_ge(scaled, CH * b)
                broadcast(RSTD2_BANK, rn3[:]).then_inc(bc3_done, 1)

            def dft_uv(n):
                pe.wait_ge(negb_ready, 1)
                for m in range(CH):
                    for c in range(CH):
                        cols = slice((m * CH + c) * P, (m * CH + c + 1) * P)
                        for s, (a, f) in enumerate((((0, 0), (1, 1)), ((0, 1), (2, 0)))[n]):
                            src = freq_sb[:, a] if a < 2 else neg_b_sb
                            mm = nc.tensor.matmul(ps[:, DFT_U_BANK + n, cols], src[:, c, m * P:(m + 1) * P],
                                                  dft_sb[:, f, c, :], start=(s == 0), stop=(s == 1))
                mm.then_inc(uv_done, 1)

            def dft_m():
                pe.wait_ge(uv_ready, 2 * 2)
                pe.wait_ge(hc1_ready, B)
                for m in range(CH):
                    for c in range(CH):
                        cols = slice((m * CH + c) * P, (m * CH + c + 1) * P)
                        for f in range(2):
                            mm = nc.tensor.matmul(ps[:, DFT_M_BANK, cols], uv[:, f, c, m * P:(m + 1) * P],
                                                  dft_sb[:, f, c, :], start=(f == 0), stop=(f == 1))
                mm.then_inc(m_done, 1)

            def qkv(b, j):
                n = (TT + CH) * b + j
                bank = QKV_BANKS[n % 4]
                if j == 0:
                    pe.wait_ge(xnlo_ready, b + 1)
                if n == 0:
                    pe.wait_ge(wlo_ready, QKV + 1)
                if n < 2:
                    pe.wait_ge(h_ready, CH * (B - 1) + n + 1)
                elif n < 4:
                    pe.wait_ge(uv_raw, n - 1)
                else:
                    pb, pj = divmod(n - 4, TT + CH)
                    if pj < TT:
                        pe.wait_ge(v_ready, TT * pb + pj + 1)
                    else:
                        pe.wait_ge(qsq_ready, CH * pb + pj - TT + 1)
                for c in range(CH):
                    if j < TT:
                        rows = slice(j * P, (j + 1) * P)
                        nc.tensor.matmul(ps[:, bank, :], xn_hi[:, b, c, rows], qkv_hi[:, c, C:3 * C],
                                         start=(c == 0), stop=False)
                        nc.tensor.matmul(ps[:, bank, :], xn_hi[:, b, c, rows], qkv_lo[:, c, C:3 * C],
                                         start=False, stop=False)
                        mm = nc.tensor.matmul(ps[:, bank, :], xn_lo[:, b, c, rows], qkv_hi[:, c, C:3 * C],
                                              start=False, stop=(c == CH - 1))
                    else:
                        o = slice((j - TT) * P, (j - TT + 1) * P)
                        mm = split_mm(ps[:, bank, :], qkv_hi[:, c, o], qkv_lo[:, c, o], xn_hi[:, b, c, :],
                                      xn_lo[:, b, c, :], c == 0, c == CH - 1)
                mm.then_inc(qkv_done, 1)

            def kv(b):
                pe.wait_ge(k_ready, b + 1)
                pe.wait_ge(v_ready, TT * (b + 1))
                if b == 0:
                    pe.wait_ge(m_raw, 1)
                    pe.wait_ge(v_ones, 2)
                else:
                    pe.wait_ge(glo_ready, b)
                r = b % 2
                for c in range(CH):
                    for t in range(TT):
                        mm = nc.tensor.matmul(ps[:, KV_BANK, c * (P + 1):(c + 1) * (P + 1)],
                                              k[:, r, t, c * P:(c + 1) * P], v[:, r, t, c, :],
                                              start=(t == 0), stop=(t == TT - 1))
                mm.then_inc(kv_done, 1)

            def kv_turn(b):
                pe.wait_ge(kvm_ready, b + 1)
                for c in range(CH):
                    mm = nc.tensor.transpose(ps[:, KV_BANK, c * P:(c + 1) * P], kv_masked[:, c, :], ident[:])
                mm.then_inc(kvt_done, 1)

            def denominators(b):
                pe.wait_ge(kvm_ready, b + 1)
                pe.wait_ge(q_ready, b + 1)
                if b == 0:
                    pe.wait_ge(st1_ready, B)
                elif b == 1:
                    pe.wait_ge(den_ready, 1)
                else:
                    pe.wait_ge(st2_ready, b - 1)
                for t in range(TT):
                    for c in range(CH):
                        col = DEN_COL + (t * CH + c) * HPH
                        mm = nc.tensor.matmul(ps[:, STAT_BANK, col:col + HPH], q[:, b % 2, c, t * P:(t + 1) * P],
                                              ksum_masked[:, c, :], start=True, stop=True)
                mm.then_inc(den_done, 1)

            def z_channels(b):
                pe.wait_ge(zx_ready, b + 1)
                if b == 0:
                    pe.wait_ge(xn_ready, B)
                    pe.wait_ge(u_ready, B)
                else:
                    pe.wait_ge(x1_ready, CH * b)
                for c in range(CH):
                    for t in range(TT):
                        mm = nc.tensor.transpose(ps[:, Z_BANK + c, t * P:(t + 1) * P],
                                                 zx[:, (t * CH + c) * P:(t * CH + c + 1) * P], ident[:])
                mm.then_inc(zt_done, 1)

            def kv_proj(b):
                pe.wait_ge(kvt_ready, b + 1)
                if b == 0:
                    pe.wait_ge(proj_in, 16)
                for c in range(CH):
                    mm = nc.tensor.matmul(ps[:, KV_BANK, c * C:(c + 1) * C], kvt[:, c, :], proj[:, c, :],
                                          start=True, stop=True)
                mm.then_inc(g_done, 1)

            def attention(b):
                pe.wait_ge(glo_ready, b + 1)
                pe.wait_ge(ghi_ready, b + 1)
                pe.wait_ge(qzlo_ready, b + 1)
                for o in range(CH):
                    for c in range(CH):
                        cols = slice(o * P, (o + 1) * P)
                        mm = split_mm(ps[:, Z_BANK + o, :], g_hi[:, c, cols], g_lo[:, c, cols],
                                      qz_hi[:, b % 2, c, :], qz_lo[:, b % 2, c, :], c == 0, c == CH - 1)
                    mm.then_inc(attn_done, 1)

            def conv1(b, j):
                n = HT * b + j
                if j == 0:
                    pe.wait_ge(xn2lo_ready, b + 1)
                if n == 0:
                    pe.wait_ge(wlo_ready, CONV1 + 1)
                if n < 2:
                    pe.wait_ge(qsq_ready, CH * B)
                else:
                    pe.wait_ge(gelu_ready, n - 1)
                for c in range(CH):
                    cols = slice(j * P, (j + 1) * P)
                    mm = split_mm(ps[:, CONV1_BANK + n % 2, :], c1_hi[:, c, cols], c1_lo[:, c, cols],
                                  xn_hi[:, b, c, :], xn_lo[:, b, c, :], c == 0, c == CH - 1)
                mm.then_inc(c1_done, 1)

            def conv2(b, o):
                if b == 0:
                    pe.wait_ge(wlo_ready, CONV2 + 1)
                    pe.wait_ge(x1_ready, CH * (B - 1) + o + 1)
                else:
                    pe.wait_ge(h1_ready, CH * (b - 1) + o + 1)
                for j in range(HT):
                    if o == 0:
                        pe.wait_ge(gelo_ready, HT * b + j + 1)
                    cols = slice(o * P, (o + 1) * P)
                    mm = split_mm(ps[:, CONV2_BANK + o, :], c2_hi[:, j, cols], c2_lo[:, j, cols],
                                  ghi[:, b % 2, j, :], glo[:, b % 2, j, :], j == 0, j == HT - 1)
                mm.then_inc(c2_done, 1)

            def ffn(b, o):
                if o == 0:
                    pe.wait_ge(nlo_ready, b + 1)
                if b == 0:
                    pe.wait_ge(mlo_ready, 1)
                    if o == 0:
                        pe.wait_ge(xn2_ready, B)
                    else:
                        pe.wait_ge(glo_ready, B)
                elif b == 1:
                    pe.wait_ge(ffn_taken, o + 1)
                elif b == 2:
                    pe.wait_ge(h1_ready, CH * (B - 1) + o + 1)
                elif o == 0:
                    pe.wait_ge(gelu_ready, HT * B)
                else:
                    pe.wait_ge(hc3_ready, B)
                for c in range(CH):
                    cols = slice(o * P, (o + 1) * P)
                    mm = split_mm(ps[:, FFN_BANKS[b][o], :], m_hi[:, c, cols], m_lo[:, c, cols],
                                  xn_hi[:, b, c, :], xn_lo[:, b, c, :], c == 0, c == CH - 1)
                mm.then_inc(ffn_done, 1)

            def first_tok_mix(d):
                pe.wait_ge(wtok_lo_ready, d + 1)
                order = [(i, o) for i in range(CH) for o in range(CH)]
                if d == D - 1:
                    pe.wait_ge(xlo_ready, d + 1)
                    order = [(i, o) for o in range(CH) for i in range(CH)]
                else:
                    pe.wait_ge(first_lo_ready, d + 1)
                for i, o in order:
                    if (i, o) == (1, 0):
                        pe.wait_ge(xlo_ready, d + 1)
                    wc = slice(i * C + o * P, i * C + o * P + P)
                    mm = split_mm(ps[:, TOK_BANK + o, :], wtok_hi[:, d, wc], wtok_lo[:, d, wc],
                                  xhi_ring[:, d, i * T:(i + 1) * T], xlo_ring[:, d, i * T:(i + 1) * T],
                                  d == 0 and i == 0, d == D - 1 and i == CH - 1)
                    if d == D - 1 and (i, o) == (CH - 1, 0):
                        mm.then_inc(tok_half0, 1)
                mm.then_inc(tok_chunk, 1)

            def mean1(b):
                pe.wait_ge(hsum1_ready, b + 1)
                if b >= 1:
                    pe.wait_ge(hc1_ready, b)
                nc.tensor.matmul(ps[:, MEAN1_BANK, :], mean_w[:], hsum[:], start=True, stop=True).then_inc(mean1_done, 1)

            def ss1(b):
                if b >= 1:
                    pe.wait_ge(st1_ready, b)
                square_sums(b, sq, sqsum1_ready, SS1_COL, ss1_done)

            def ss2(b):
                if b + 2 <= B:
                    pe.wait_ge(den_ready, b + 2)
                if b == B - 1:
                    pe.wait_ge(st2_ready, b)
                square_sums(b, sq2, sqsum2_ready, SS2_COL, ss2_done)

            def mean3(b):
                pe.wait_ge(hsum3_ready, b + 1)
                if b == 0:
                    pe.wait_ge(v_ready, TT * B)
                elif b == 1:
                    pe.wait_ge(scaled, CH)
                elif b == 2:
                    pe.wait_ge(gelu_ready, HT * B - 1)
                else:
                    pe.wait_ge(hc3_ready, b)
                nc.tensor.matmul(ps[:, MEAN2_BANKS[b], :], mean_w[:], hsum[:], start=True, stop=True).then_inc(mean3_done, 1)

            def ss3(b):
                if b == 0:
                    pe.wait_ge(st2_ready, B)
                else:
                    pe.wait_ge(st3_ready, b)
                square_sums(b, sq, sqsum3_ready, SS3_COL, ss3_done)

            pe.wait_ge(consts_ready, 1)
            for _ in range(WARM_UP):
                nc.tensor.matmul(ps[:, DFT_V_BANK, 0:P], mean_w[:], mean_w[:], start=True, stop=True)
            pe.wait_ge(consts_ready, 5)
            for d in range(D):
                first_tok_mix(d)
            for b in range(1, B):
                tok_mix(b, 0)
                mean1(b - 1)
                tok_mix(b, 1)
                tok_mix(b, 2, (0,))
                ss1(b - 1)
                tok_mix(b, 2, (1,))
                tok_mix(b, 3)
                bc1(b - 1)
            dft_uv(0)
            mean1(3)
            dft_uv(1)
            for j in range(TT):
                qkv(0, j)
            ss1(3)
            dft_m()
            bc1(3)
            qkv(0, 4)
            qkv(0, 5)
            for b in range(1, B):
                qkv(b, 0)
                qkv(b, 1)
                kv(b - 1)
                if b == 3:
                    ss2(0)
                qkv(b, 2)
                kv_turn(b - 1)
                denominators(b - 1)
                if b >= 2:
                    attention(b - 2)
                qkv(b, 3)
                kv_proj(b - 1)
                z_channels(b - 1)
                if b == 3:
                    bc2(0)
                qkv(b, 4)
                if b == 3:
                    ss2(1)
                qkv(b, 5)
            kv(3)
            attention(2)
            kv_turn(3)
            bc2(1)
            conv1(0, 0)
            denominators(3)
            conv1(0, 1)
            kv_proj(3)
            ss2(2)
            conv1(0, 2)
            z_channels(3)
            conv1(0, 3)
            conv1(1, 0)
            bc2(2)
            conv1(1, 1)
            attention(3)
            conv1(1, 2)
            conv1(1, 3)
            conv2(0, 0)
            conv2(0, 1)
            ss2(3)
            conv1(2, 0)
            bc2(3)
            conv1(2, 1)
            conv1(2, 2)
            mean3(0)
            conv1(2, 3)
            conv2(1, 0)
            conv2(1, 1)
            ss3(0)
            conv1(3, 0)
            conv1(3, 1)
            bc3(0)
            ffn(0, 0)
            ffn(0, 1)
            conv1(3, 2)
            conv1(3, 3)
            mean3(1)
            conv2(2, 0)
            conv2(2, 1)
            ss3(1)
            conv2(3, 0)
            mean3(2)
            bc3(1)
            conv2(3, 1)
            ffn(1, 0)
            ss3(2)
            mean3(3)
            ffn(1, 1)
            ffn(2, 0)
            ffn(2, 1)
            bc3(2)
            ss3(3)
            ffn(3, 0)
            bc3(3)
            ffn(3, 1)

        @block.scalar
        def _(act):
            def copy(dst, src, done):
                nc.scalar.activation(dst, src, ACT.Copy).then_inc(done, 1)

            def wtok_split(d):
                act.wait_ge(wtok_ready, d + 1)
                copy(wtok_hi[:, d, :], wtok[:, d, :], wtok_hi_ready)

            def x_split(b, d):
                act.wait_ge(x_in[d], 16 * (b + 1))
                if b >= 1:
                    act.wait_ge(tok_chunk, D * (b - 1) + d + 1)
                copy(xhi_ring[:, d, :], x_ring[:, d, :], xhi_ready)

            def first_x_split(d):
                act.wait_ge(x_in[d], 16)
                copy(xhi_ring[:, d, 0:T], x_ring[:, d, 0:T], first_hi_ready)
                copy(xhi_ring[:, d, T:2 * T], x_ring[:, d, T:2 * T], xhi_ready)

            def h_out(b):
                for o in range(CH):
                    if o == 0:
                        act.wait_ge(tok_half0, b + 1)
                    else:
                        act.wait_ge(tok_chunk, D * (b + 1))
                    copy(h[:, o, b * T:(b + 1) * T], ps[:, TOK_BANK + o, :], h_ready)

            def square1(b):
                act.wait_ge(hc1_ready, b + 1)
                if b >= 1:
                    act.wait_ge(ss1_done, b)
                nc.scalar.activation(sq[:], tok(u, b), ACT.Square).then_inc(sq1_ready, 1)

            def xn_split(b):
                act.wait_ge(xn_ready, b + 1)
                copy(xn_hi[:, b], xn[:], xnhi_ready)

            def weight_split(n, dst, src):
                if n == CONV2:
                    act.wait_ge(c2_in, 16)
                else:
                    act.wait_ge(wscaled, n + 1)
                copy(dst, src, whi_ready)

            def k_square(b, t):
                act.wait_ge(qkv_done, (TT + CH) * b + t + 1)
                if b >= 2:
                    act.wait_ge(kv_done, b - 1)
                if b == 0 and t == 0:
                    act.wait_ge(m_done, 1)
                nc.scalar.activation(k[:, b % 2, t, :], ps[:, QKV_BANKS[((TT + CH) * b + t) % 4], 0:C],
                                     ACT.Square).then_inc(ksq_ready, 1)

            def k_exp(b):
                act.wait_ge(ksq_ready, TT * (b + 1))
                nc.scalar.activation(k[:, b % 2], k[:, b % 2], ACT.Exp, scale=-0.5).then_inc(k_ready, 1)

            def q_square(b, o):
                act.wait_ge(qkv_done, (TT + CH) * b + TT + o + 1)
                if b >= 2:
                    act.wait_ge(qzlo_ready, b - 1)
                elif b == 0 and o == 0:
                    act.wait_ge(wlo_ready, CONV2 + 1)
                nc.scalar.activation(q[:, b % 2, o, :], ps[:, QKV_BANKS[((TT + CH) * b + TT + o) % 4], :],
                                     ACT.Square).then_inc(qsq_ready, 1)

            def q_exp(b):
                act.wait_ge(qsq_ready, CH * (b + 1))
                nc.scalar.activation(q[:, b % 2], q[:, b % 2], ACT.Exp, scale=-0.5).then_inc(q_ready, 1)

            def z_expand(b):
                act.wait_ge(z_ready, b + 1)
                if b >= 1:
                    act.wait_ge(zt_done, b)
                copy(zx.rearrange("p (h d) -> p h d", d=DH),
                     z[:].unsqueeze(2).to_broadcast([P, TT * CH * HPH, DH]), zx_ready)

            def g_split(b):
                act.wait_ge(g_done, b + 1)
                if b >= 1:
                    act.wait_ge(attn_done, CH * b)
                copy(g_hi[:].rearrange("p c n -> p (c n)"), ps[:, KV_BANK, :], ghi_ready)

            def qz_split(b):
                act.wait_ge(qz_ready, b + 1)
                if b >= 2:
                    act.wait_ge(attn_done, CH * (b - 1))
                copy(qz_hi[:, b % 2], q[:, b % 2], qzhi_ready)

            def square2(b):
                act.wait_ge(x1_ready, CH * (b + 1))
                if b >= 1:
                    act.wait_ge(ss2_done, b)
                nc.scalar.activation(sq2, tok(u, b), ACT.Square).then_inc(sq2_ready, 1)

            def xn2_split(b):
                act.wait_ge(xn2_ready, b + 1)
                copy(xn_hi[:, b], xn2, xn2hi_ready)

            def gelu(b, j):
                act.wait_ge(c1_done, HT * b + j + 1)
                if b >= 1:
                    act.wait_ge(gelo_ready, HT * (b - 1) + j + 1)
                nc.scalar.activation(g[:, j, :], ps[:, CONV1_BANK + (HT * b + j) % 2, :], ACT.Gelu,
                                     bias=vecs[:, V_CONV1B + j:V_CONV1B + j + 1]).then_inc(gelu_ready, 1)

            def gelu_hi(b, j):
                act.wait_ge(gelu_ready, HT * b + j + 1)
                if b >= 2:
                    act.wait_ge(c2_done, CH * (b - 1))
                copy(ghi[:, b % 2, j, :], g[:, j, :], gehi_ready)

            def square3(b):
                act.wait_ge(hc3_ready, b + 1)
                if b >= 1:
                    act.wait_ge(ss3_done, b)
                nc.scalar.activation(sq[:], hc[:], ACT.Square).then_inc(sq3_ready, 1)

            def h1_split(b):
                act.wait_ge(h1_ready, CH * (b + 1))
                copy(xn_hi[:, b], tok(h, b), nhi_ready)

            def ffn_out(b, o):
                act.wait_ge(ffn_done, CH * b + o + 1)
                if b == 0 and o == 0:
                    act.wait_ge(xn2lo_ready, B)
                elif b == 1 and o == 0:
                    act.wait_ge(ss2_done, B)
                elif b >= 2:
                    act.wait_ge(out_ready, CH * (b - 2) + o + 1)
                copy(fout[b % 2][:, o, :], ps[:, FFN_BANKS[b][o], :], ffn_taken)

            def uv_out(n):
                act.wait_ge(uv_done, n + 1)
                copy(uv_parts[:, n].rearrange("p m c n -> p (m c n)"), ps[:, DFT_U_BANK + n, :], uv_raw)

            def m_out():
                act.wait_ge(m_done, 1)
                nc.scalar.activation(m_parts.rearrange("p m c n -> p (m c n)"), ps[:, DFT_M_BANK, :], ACT.Copy,
                                     scale=1.0 / C).then_inc(m_raw, 1)

            def m_split():
                act.wait_ge(m_ready, 2)
                copy(m_hi[:], m_full, mhi_ready)

            for d in range(D):
                wtok_split(d)
                first_x_split(d)
            for d in range(3):
                x_split(1, d)
            for b in range(B):
                h_out(b)
                if b + 1 < B:
                    x_split(b + 1, 3)
                if b == 3:
                    uv_out(0)
                if b >= 1:
                    xn_split(b - 1)
                if b == 3:
                    uv_out(1)
                square1(b)
                if b == 3:
                    weight_split(CONV2, c2_hi[:].rearrange("p c n -> p (c n)"), stage[:, 0:HT * C])
                if b + 2 < B:
                    x_split(b + 2, 0)
                if b + 2 < B:
                    x_split(b + 2, 1)
                if b == 0:
                    weight_split(QKV, qkv_hi[:].rearrange("p c n -> p (c n)"), stage[:, 0:CH * 3 * C])
                if b == 2:
                    weight_split(CONV1, c1_hi[:].rearrange("p c n -> p (c n)"), stage[:, 0:CH * HID])
                if b + 2 < B:
                    x_split(b + 2, 2)
            k_square(0, 0)
            m_out()
            k_square(0, 1)
            k_square(0, 2)
            k_square(0, 3)
            k_exp(0)
            xn_split(3)
            q_square(0, 0)
            m_split()
            q_square(0, 1)
            q_exp(0)
            for b in range(1, B):
                k_square(b, 0)
                k_square(b, 1)
                k_square(b, 2)
                z_expand(b - 1)
                k_square(b, 3)
                if b == 3:
                    square2(1)
                g_split(b - 1)
                k_exp(b)
                if b == 2:
                    square2(0)
                qz_split(b - 1)
                q_square(b, 0)
                q_square(b, 1)
                q_exp(b)

            def gelus(b, *tiles):
                for j in tiles:
                    gelu(b, j)
                    gelu_hi(b, j)

            xn2_split(0)
            square2(2)
            gelus(0, 0)
            z_expand(3)
            xn2_split(1)
            gelus(0, 1)
            g_split(3)
            gelus(0, 2)
            qz_split(3)
            gelus(0, 3)
            gelus(1, 0)
            xn2_split(2)
            gelus(1, 1)
            square2(3)
            gelus(1, 2, 3)
            gelus(2, 0)
            xn2_split(3)
            gelus(2, 1)
            h1_split(0)
            gelus(2, 2)
            square3(0)
            gelus(2, 3)
            gelus(3, 0)
            h1_split(1)
            gelus(3, 1)
            ffn_out(0, 0)
            ffn_out(0, 1)
            gelus(3, 2, 3)
            square3(1)
            h1_split(2)
            square3(2)
            h1_split(3)
            ffn_out(1, 0)
            square3(3)
            ffn_out(1, 1)
            for b in (2, 3):
                for o in range(CH):
                    ffn_out(b, o)

        @block.gpsimd
        def _(pool):
            def constants():
                nc.gpsimd.memset(mean_w[:], 1.0 / C).then_inc(consts_ready, 1)
                nc.gpsimd.memset(ones[:], 1.0).then_inc(consts_ready, 1)
                nc.gpsimd.memset(minus_half[:], -0.5).then_inc(consts_ready, 1)
                nc.gpsimd.memset(ident[:], 0.0).then_inc(id_zeroed, 1)
                nc.gpsimd.memset(headmask[:], 1.0).then_inc(mask_step, 1)
                pool.wait_ge(id_zeroed, 1)
                nc.gpsimd.affine_select(out=ident[:], in_=ident[:], compare_op=ALU.not_equal, fill=1.0, base=0,
                                        pattern=[[-1, P]], channel_multiplier=1).then_inc(consts_ready, 1)
                m3 = headmask[:].rearrange("p (a d) -> p a d", d=DH)
                pool.wait_ge(mask_step, 1)
                nc.gpsimd.affine_select(out=m3, in_=m3, compare_op=ALU.is_ge, fill=0.0, base=0,
                                        pattern=[[-DH, HPH], [0, DH]], channel_multiplier=1).then_inc(mask_step, 1)
                pool.wait_ge(mask_step, 2)
                nc.gpsimd.affine_select(out=m3, in_=m3, compare_op=ALU.is_ge, fill=0.0, base=DH - 1,
                                        pattern=[[DH, HPH], [0, DH]], channel_multiplier=-1).then_inc(consts_ready, 1)

            def wtok_lo_split(d):
                pool.wait_ge(wtok_hi_ready, d + 1)
                nc.gpsimd.tensor_tensor(wtok_lo[:, d, :], wtok[:, d, :], wtok_hi[:, d, :].bitcast(F32),
                                        ALU.subtract).then_inc(wtok_lo_ready, 1)

            def gains():
                pool.wait_ge(vec_in, 16)
                nc.gpsimd.tensor_scalar(gain[:], vecs[:, V_SCALE1:V_SCALE1 + 4], RMS_GAIN, 1.0, ALU.mult,
                                        ALU.mult).then_inc(gains_ready, 1)
                for n, col in enumerate((V_PROJB, V_CONV2B)):
                    nc.gpsimd.tensor_tensor(gbias[:, 2 * n:2 * n + 2], vecs[:, col:col + 2],
                                            vecs[:, V_GAMMA:V_GAMMA + 2], ALU.mult).then_inc(gains_ready, 1)

            def scale_weights(n, width, loaded):
                pool.wait_ge(loaded, 16)
                for c in range(CH):
                    rows = stage[:, c * width:(c + 1) * width]
                    last = nc.gpsimd.tensor_scalar(rows, rows, gain[:, 2 * n + c:2 * n + c + 1], 1.0, ALU.mult,
                                                   ALU.mult)
                last.then_inc(wscaled, 1)

            def weight_lo(n, dst, hi, src):
                pool.wait_ge(whi_ready, n + 1)
                nc.gpsimd.tensor_tensor(dst, src, hi.bitcast(F32), ALU.subtract).then_inc(wlo_ready, 1)

            def rn1_pow(b):
                for n in range(2):
                    pool.wait_ge(st1_ready, b + 1)
                    if b >= 1:
                        pool.wait_ge(bc1_done, 2 * (b - 1) + n + 1)
                    cols = slice(n * TT, (n + 1) * TT)
                    nc.gpsimd.tensor_tensor(rn1[:, cols], st1[:, cols], minus_half[:, cols],
                                            ALU.pow).then_inc(rn1_ready, 1)

            def u_bias(b):
                pool.wait_ge(u_ready, b + 1)
                for c in range(CH):
                    a = u[:, c, b * T:(b + 1) * T]
                    nc.gpsimd.tensor_scalar(a, a, gbias[:, c:c + 1], 1.0, ALU.add, ALU.mult).then_inc(ub_ready, 1)

            def xn_lo_split(b):
                pool.wait_ge(xnhi_ready, b + 1)
                nc.gpsimd.tensor_tensor(xn_lo[:, b], xn[:], xn_hi[:, b].bitcast(F32),
                                        ALU.subtract).then_inc(xnlo_ready, 1)

            def rn_pow(b, st, ready, rn, used, done):
                pool.wait_ge(ready, b + 1)
                if b >= 1:
                    pool.wait_ge(used, b)
                nc.gpsimd.tensor_tensor(rn[:], st[:], minus_half[:, 0:TT], ALU.pow).then_inc(done, 1)

            def square_sum(b, squares, ready, done):
                pool.wait_ge(ready, b + 1)
                nc.gpsimd.tensor_tensor(squares[:, 0, :], squares[:, 0, :], squares[:, 1, :], ALU.add).then_inc(done, 1)

            def rn2_pow(b):
                rn_pow(b, st2, st2_ready, rn2, bc2_done, rn2_ready)

            def rn3_pow(b):
                rn_pow(b, st3, st3_ready, rn3, bc3_done, rn3_ready)

            def last_h1_lo_split():
                b = B - 1
                pool.wait_ge(nhi_ready, b + 1)
                nc.gpsimd.tensor_tensor(xn_lo[:, b], tok(h, b), xn_hi[:, b].bitcast(F32),
                                        ALU.subtract).then_inc(nlo_ready, 1)

            constants()
            for d in range(1, D):
                wtok_lo_split(d)
            gains()
            pool.wait_ge(gains_ready, 3)
            scale_weights(QKV, 3 * C, qkv_in)
            for b in range(B):
                square_sum(b, sq, sq1_ready, sqsum1_ready)
                rn1_pow(b)
                if b == 0:
                    weight_lo(QKV, qkv_lo[:].rearrange("p c n -> p (c n)"), qkv_hi[:].rearrange("p c n -> p (c n)"),
                              stage[:, 0:CH * 3 * C])
                if b == 1:
                    scale_weights(CONV1, HID, c1_in)
                if b == 2:
                    weight_lo(CONV1, c1_lo[:].rearrange("p c n -> p (c n)"), c1_hi[:].rearrange("p c n -> p (c n)"),
                              stage[:, 0:CH * HID])
                if b == 3:
                    weight_lo(CONV2, c2_lo[:].rearrange("p c n -> p (c n)"), c2_hi[:].rearrange("p c n -> p (c n)"),
                              stage[:, 0:HT * C])
                if b >= 1:
                    u_bias(b - 1)
            pool.wait_ge(m_done, 1)
            for r in range(2):
                nc.gpsimd.memset(v[:, r, :, :, P:P + 1], 1.0).then_inc(v_ones, 1)
            xn_lo_split(3)
            u_bias(3)
            for b in range(B):
                square_sum(b, sq2, sq2_ready, sqsum2_ready)
                rn2_pow(b)
            for b in range(B):
                square_sum(b, sq, sq3_ready, sqsum3_ready)
                if b == 2:
                    last_h1_lo_split()
                rn3_pow(b)

        @block.vector
        def _(dve):
            def wtok_build(d):
                if d == 1:
                    dve.wait_ge(w_rest_in, 16)
                for c in range(CH):
                    last = nc.vector.tensor_tensor(wtok[:, d, c * C:(c + 1) * C], ws_sb[:, c * C:(c + 1) * C],
                                                   w_bc[:, d, :], ALU.mult)
                last.then_inc(wtok_ready, 1)

            def first_wtok_lo_split():
                dve.wait_ge(wtok_hi_ready, 1)
                nc.vector.tensor_tensor(wtok_lo[:, 0, :], wtok[:, 0, :], wtok_hi[:, 0, :].bitcast(F32),
                                        ALU.subtract).then_inc(wtok_lo_ready, 1)

            def x_lo_split(b, d):
                dve.wait_ge(xhi_ready, D * b + d + 1)
                nc.vector.tensor_tensor(xlo_ring[:, d, :], x_ring[:, d, :], xhi_ring[:, d, :].bitcast(F32),
                                        ALU.subtract).then_inc(xlo_ready, 1)

            def first_x_lo_split(d):
                for n, hi_ready, lo_ready in ((0, first_hi_ready, first_lo_ready), (1, xhi_ready, xlo_ready)):
                    cols = slice(n * T, (n + 1) * T)
                    dve.wait_ge(hi_ready, d + 1)
                    nc.vector.tensor_tensor(xlo_ring[:, d, cols], x_ring[:, d, cols], xhi_ring[:, d, cols].bitcast(F32),
                                            ALU.subtract).then_inc(lo_ready, 1)

            def hsum1(b):
                dve.wait_ge(h_ready, CH * (b + 1))
                if b >= 1:
                    dve.wait_ge(mean1_done, b)
                nc.vector.tensor_tensor(hsum[:], h[:, 0, b * T:(b + 1) * T], h[:, 1, b * T:(b + 1) * T],
                                        ALU.add).then_inc(hsum1_ready, 1)

            def mean_bank(bank):
                return ps[:, bank:bank + 1, :].to_broadcast([P, CH, T])

            def center1(b):
                dve.wait_ge(mean1_done, b + 1)
                nc.vector.tensor_tensor(tok(u, b), tok(h, b), mean_bank(MEAN1_BANK), ALU.subtract).then_inc(hc1_ready, 1)

            def stats1(b):
                dve.wait_ge(ss1_done, b + 1)
                if b >= 1:
                    dve.wait_ge(rn1_ready, 2 * b)
                nc.vector.tensor_copy(st1[:, 0:TT], ps[:, STAT_BANK, SS1_COL:SS1_COL + TT])
                nc.vector.tensor_scalar(st1[:, TT:2 * TT], ps[:, STAT_BANK, SS1_COL:SS1_COL + TT], 1.0 / C, LN_EPS,
                                        ALU.mult, ALU.add).then_inc(st1_ready, 1)

            def rmsnorm1(b):
                dve.wait_ge(bc1_done, 2 * b + 1)
                if b >= 1:
                    dve.wait_ge(xnlo_ready, b)
                nc.vector.tensor_tensor(xn[:], tok(u, b), mean_bank(RNORM_BANK), ALU.mult).then_inc(xn_ready, 1)

            def layernorm1(b):
                dve.wait_ge(sq1_ready, b + 1)
                dve.wait_ge(xn_ready, b + 1)
                dve.wait_ge(bc1_done, 2 * b + 2)
                nc.vector.tensor_tensor(tok(u, b), tok(u, b), mean_bank(RSTD_BANK), ALU.mult).then_inc(u_ready, 1)

            def xn_lo_split(b):
                dve.wait_ge(xnhi_ready, b + 1)
                nc.vector.tensor_tensor(xn_lo[:, b], xn[:], xn_hi[:, b].bitcast(F32),
                                        ALU.subtract).then_inc(xnlo_ready, 1)

            def neg_b():
                dve.wait_ge(dft_in, 32)
                nc.vector.tensor_scalar(neg_b_sb, freq_sb[:, 1], -1.0, None, ALU.mult).then_inc(negb_ready, 1)

            def uv_center(n):
                a = uv_parts[:, n]
                dve.wait_ge(uv_raw, n + 1)
                nc.vector.reduce_sum(row_sum[:, n], a[:, :, 0, :], axis=mybir.AxisListType.X).then_inc(uv_sum, 1)
                dve.wait_ge(uv_sum, n + 1)
                nc.vector.tensor_scalar(row_mean[:, n], row_sum[:, n], 2.0 / C, None, ALU.mult).then_inc(uv_mean, 1)
                dve.wait_ge(uv_mean, n + 1)
                nc.vector.tensor_tensor(a[:, :, 0, :], a[:, :, 0, :],
                                        row_mean[:, n].unsqueeze(2).to_broadcast([P, CH, P]),
                                        ALU.subtract).then_inc(uv_centered, 1)
                dve.wait_ge(uv_centered, n + 1)
                for half, op in enumerate((ALU.add, ALU.subtract)):
                    nc.vector.tensor_tensor(uv[:, n, :, half * P:(half + 1) * P], a[:, :, 0, :], a[:, :, 1, :],
                                            op).then_inc(uv_ready, 1)

            def m_join():
                dve.wait_ge(m_raw, 1)
                for half, op in enumerate((ALU.add, ALU.subtract)):
                    nc.vector.tensor_tensor(m_full[:, :, half * P:(half + 1) * P], m_parts[:, :, 0, :],
                                            m_parts[:, :, 1, :], op).then_inc(m_ready, 1)

            def m_lo_split():
                dve.wait_ge(mhi_ready, 1)
                nc.vector.tensor_tensor(m_lo[:], m_full, m_hi[:].bitcast(F32), ALU.subtract).then_inc(mlo_ready, 1)

            def v_copy(b, t):
                dve.wait_ge(ksq_ready, TT * b + t + 1)
                if b >= 2:
                    dve.wait_ge(kv_done, b - 1)
                bank = QKV_BANKS[((TT + CH) * b + t) % 4]
                nc.vector.tensor_copy(v[:, b % 2, t, :, 0:P],
                                      ps[:, bank, C:2 * C].rearrange("p (c n) -> p c n", c=CH)).then_inc(v_ready, 1)

            def kv_mask(b):
                dve.wait_ge(kv_done, b + 1)
                if b >= 1:
                    dve.wait_ge(kvt_done, b)
                    dve.wait_ge(den_done, b)
                else:
                    dve.wait_ge(consts_ready, 5)
                kv_ps = ps[:, KV_BANK, 0:CH * (P + 1)].rearrange("p (c n) -> p c n", c=CH)
                nc.vector.tensor_tensor(kv_masked[:], kv_ps[:, :, 0:P], headmask[:].unsqueeze(1).to_broadcast([P, CH, P]),
                                        ALU.mult)
                for c in range(CH):
                    last = nc.vector.tensor_scalar(ksum_masked[:, c, :], headmask[:, 0:P:DH], kv_ps[:, c, P:P + 1],
                                                   None, ALU.mult)
                last.then_inc(kvm_ready, 1)

            def kvt_out(b):
                dve.wait_ge(kvt_done, b + 1)
                if b >= 1:
                    dve.wait_ge(g_done, b)
                nc.vector.tensor_copy(kvt[:].rearrange("p c n -> p (c n)"), ps[:, KV_BANK, 0:C]).then_inc(kvt_ready, 1)

            def reciprocals(b):
                dve.wait_ge(den_done, b + 1)
                nc.vector.tensor_scalar(den[:], ps[:, STAT_BANK, DEN_COL:DEN_COL + TT * CH * HPH], DEN_EPS, None,
                                        ALU.add).then_inc(den_ready, 1)
                dve.wait_ge(den_ready, b + 1)
                if b >= 1:
                    dve.wait_ge(zx_ready, b)
                nc.vector.reciprocal(z[:], den[:]).then_inc(z_ready, 1)

            def scale_q(b):
                dve.wait_ge(zt_done, b + 1)
                nc.vector.tensor_tensor(q[:, b % 2], q[:, b % 2], ps[:, Z_BANK:Z_BANK + CH, :],
                                        ALU.mult).then_inc(qz_ready, 1)

            def qz_lo_split(b):
                dve.wait_ge(qzhi_ready, b + 1)
                nc.vector.tensor_tensor(qz_lo[:, b % 2], q[:, b % 2], qz_hi[:, b % 2].bitcast(F32),
                                        ALU.subtract).then_inc(qzlo_ready, 1)

            def g_lo_split(b):
                dve.wait_ge(ghi_ready, b + 1)
                nc.vector.tensor_tensor(g_lo[:].rearrange("p c n -> p (c n)"), ps[:, KV_BANK, :],
                                        g_hi[:].rearrange("p c n -> p (c n)").bitcast(F32),
                                        ALU.subtract).then_inc(glo_ready, 1)

            def x1(b):
                for o in range(CH):
                    dve.wait_ge(attn_done, CH * b + o + 1)
                    dve.wait_ge(ub_ready, CH * b + o + 1)
                    a = u[:, o, b * T:(b + 1) * T]
                    nc.vector.scalar_tensor_tensor(out=a, in0=ps[:, Z_BANK + o, :],
                                                   scalar=vecs[:, V_GAMMA + o:V_GAMMA + o + 1], in1=a,
                                                   op0=ALU.mult, op1=ALU.add).then_inc(x1_ready, 1)

            def stats2(b):
                dve.wait_ge(ss2_done, b + 1)
                if b >= 1:
                    dve.wait_ge(rn2_ready, b)
                nc.vector.tensor_copy(st2[:], ps[:, STAT_BANK, SS2_COL:SS2_COL + TT]).then_inc(st2_ready, 1)

            def normalize2(b):
                dve.wait_ge(bc2_done, b + 1)
                if b >= 1:
                    dve.wait_ge(xn2lo_ready, b)
                nc.vector.tensor_tensor(xn2, tok(u, b), mean_bank(RMS_BANK), ALU.mult).then_inc(xn2_ready, 1)

            def xn2_lo_split(b):
                dve.wait_ge(xn2hi_ready, b + 1)
                nc.vector.tensor_tensor(xn_lo[:, b], xn2, xn_hi[:, b].bitcast(F32), ALU.subtract).then_inc(xn2lo_ready, 1)

            def h_plus_x1(b):
                dve.wait_ge(x1_ready, CH * (b + 1))
                for o in range(CH):
                    cols = slice(b * T, (b + 1) * T)
                    nc.vector.scalar_tensor_tensor(out=h[:, o, cols], in0=u[:, o, cols], scalar=gbias[:, 2 + o:3 + o],
                                                   in1=h[:, o, cols], op0=ALU.add, op1=ALU.add).then_inc(hx_ready, 1)

            def gelu_split(b, j):
                dve.wait_ge(gehi_ready, HT * b + j + 1)
                nc.vector.tensor_tensor(glo[:, b % 2, j, :], g[:, j, :], ghi[:, b % 2, j, :].bitcast(F32),
                                        ALU.subtract).then_inc(gelo_ready, 1)

            def h1(b):
                for o in range(CH):
                    dve.wait_ge(c2_done, CH * b + o + 1)
                    dve.wait_ge(hx_ready, CH * b + o + 1)
                    a = h[:, o, b * T:(b + 1) * T]
                    nc.vector.scalar_tensor_tensor(out=a, in0=ps[:, CONV2_BANK + o, :],
                                                   scalar=vecs[:, V_GAMMA + o:V_GAMMA + o + 1], in1=a,
                                                   op0=ALU.mult, op1=ALU.add).then_inc(h1_ready, 1)

            def hsum3(b):
                dve.wait_ge(h1_ready, CH * (b + 1))
                if b >= 1:
                    dve.wait_ge(mean3_done, b)
                nc.vector.tensor_tensor(hsum[:], h[:, 0, b * T:(b + 1) * T], h[:, 1, b * T:(b + 1) * T],
                                        ALU.add).then_inc(hsum3_ready, 1)

            def center3(b):
                dve.wait_ge(mean3_done, b + 1)
                if b >= 1:
                    dve.wait_ge(sq3_ready, b)
                nc.vector.tensor_tensor(hc[:], tok(h, b), mean_bank(MEAN2_BANKS[b]), ALU.subtract).then_inc(hc3_ready, 1)

            def stats3(b):
                dve.wait_ge(ss3_done, b + 1)
                if b >= 1:
                    dve.wait_ge(rn3_ready, b)
                nc.vector.tensor_scalar(st3[:], ps[:, STAT_BANK, SS3_COL:SS3_COL + TT], 1.0 / C, LN_EPS,
                                        ALU.mult, ALU.add).then_inc(st3_ready, 1)

            def h1_lo_split(b):
                dve.wait_ge(nhi_ready, b + 1)
                nc.vector.tensor_tensor(xn_lo[:, b], tok(h, b), xn_hi[:, b].bitcast(F32),
                                        ALU.subtract).then_inc(nlo_ready, 1)

            def scale(b, o):
                a = fout[b % 2][:, o, :]
                dve.wait_ge(ffn_taken, CH * b + o + 1)
                dve.wait_ge(bc3_done, b + 1)
                nc.vector.tensor_tensor(a, a, ps[:, RSTD2_BANK, :], ALU.mult).then_inc(scaled, 1)

            def result(b, o):
                dve.wait_ge(scaled, CH * b + o + 1)
                dve.wait_ge(nlo_ready, b + 1)
                ho = h[:, o, b * T:(b + 1) * T]
                nc.vector.scalar_tensor_tensor(out=ho, in0=fout[b % 2][:, o, :],
                                               scalar=vecs[:, V_FFNB + o:V_FFNB + o + 1],
                                               in1=ho, op0=ALU.add, op1=ALU.add).then_inc(out_ready, 1)

            dve.wait_ge(ws_in, 16)
            dve.wait_ge(w_in, 16)
            wtok_build(0)
            first_wtok_lo_split()
            first_x_lo_split(0)
            wtok_build(1)
            wtok_build(2)
            first_x_lo_split(1)
            wtok_build(3)
            first_x_lo_split(2)
            first_x_lo_split(3)
            for d in range(3):
                x_lo_split(1, d)
            for b in range(B):
                hsum1(b)
                if b >= 1:
                    rmsnorm1(b - 1)
                    layernorm1(b - 1)
                center1(b)
                if b + 1 < B:
                    x_lo_split(b + 1, 3)
                if b >= 1:
                    xn_lo_split(b - 1)
                if b == 3:
                    uv_center(0)
                if b + 2 < B:
                    x_lo_split(b + 2, 0)
                if b == 3:
                    uv_center(1)
                stats1(b)
                if b + 2 < B:
                    x_lo_split(b + 2, 1)
                if b == 1:
                    neg_b()
                if b + 2 < B:
                    x_lo_split(b + 2, 2)
            v_copy(0, 0)
            v_copy(0, 1)
            m_join()
            v_copy(0, 2)
            v_copy(0, 3)
            rmsnorm1(3)
            layernorm1(3)
            m_lo_split()
            for b in range(1, B):
                v_copy(b, 0)
                v_copy(b, 1)
                kv_mask(b - 1)
                if b == 3:
                    stats2(0)
                v_copy(b, 2)
                kvt_out(b - 1)
                reciprocals(b - 1)
                if b >= 2:
                    x1(b - 2)
                v_copy(b, 3)
                g_lo_split(b - 1)
                scale_q(b - 1)
                if b == 3:
                    normalize2(0)
                qz_lo_split(b - 1)
            stats2(1)
            kv_mask(3)
            xn2_lo_split(0)
            x1(2)
            kvt_out(3)
            normalize2(1)
            reciprocals(3)
            gelu_split(0, 0)
            xn2_lo_split(1)
            gelu_split(0, 1)
            g_lo_split(3)
            scale_q(3)
            stats2(2)
            gelu_split(0, 2)
            qz_lo_split(3)
            gelu_split(0, 3)
            normalize2(2)
            xn2_lo_split(2)
            gelu_split(1, 0)
            x1(3)
            gelu_split(1, 1)
            gelu_split(1, 2)
            gelu_split(1, 3)
            h_plus_x1(0)
            stats2(3)
            h1(0)
            hsum3(0)
            normalize2(3)
            gelu_split(2, 0)
            xn2_lo_split(3)
            gelu_split(2, 1)
            h1_lo_split(0)
            center3(0)
            gelu_split(2, 2)
            h_plus_x1(1)
            gelu_split(2, 3)
            h1(1)
            hsum3(1)
            stats3(0)
            gelu_split(3, 0)
            h1_lo_split(1)
            gelu_split(3, 1)
            h_plus_x1(2)
            scale(0, 0)
            scale(0, 1)
            result(0, 0)
            result(0, 1)
            gelu_split(3, 2)
            gelu_split(3, 3)
            center3(1)
            h_plus_x1(3)
            h1(2)
            hsum3(2)
            stats3(1)
            h1_lo_split(2)
            center3(2)
            h1(3)
            hsum3(3)
            stats3(2)
            center3(3)
            scale(1, 0)
            scale(1, 1)
            result(1, 0)
            result(1, 1)
            stats3(3)
            scale(2, 0)
            scale(2, 1)
            result(2, 0)
            result(2, 1)
            scale(3, 0)
            result(3, 0)
            scale(3, 1)
            result(3, 1)


def kernel(**inputs):
    import numpy as np
    import concourse.bacc as bacc
    from concourse.bass_utils import run_bass_kernel_spmd

    def halves(a):
        n = a.shape[0] // P
        return np.ascontiguousarray(a.reshape(n, P, -1).transpose(1, 0, 2).reshape(P, -1))

    get = {name: np.asarray(a) for name, a in inputs.items()}
    x = get["x"].reshape(B, T, CH, P, D).transpose(0, 4, 3, 2, 1)
    vectors = np.concatenate([get[n].reshape(-1, P).T for n in (
        "L0_attn_scale1", "L0_attn_scale2", "L0_attn_gamma", "L0_attn_proj_b", "L0_attn_conv2_b", "L0_ffn_bias",
        "L0_attn_conv1_b")], axis=1)
    order = np.concatenate([np.arange(0, C, 2), np.arange(1, C, 2)])
    angle = 2 * np.pi * (np.outer(order, np.arange(C // 2)) % C) / C
    arrays = {
        "x": np.ascontiguousarray(x.reshape(B, D, P, CH * T)),
        "ws": halves(get["L0_tok_weighted_sum"].T),
        "w": np.ascontiguousarray(np.broadcast_to(get["L0_tok_weight"].T.reshape(1, D * C), (P, D * C))),
        "vec": np.ascontiguousarray(vectors),
        "qkv_w": halves(get["L0_attn_qkv_w"].T),
        "proj_w": halves(get["L0_attn_proj_w"].T),
        "conv1_w": halves(get["L0_attn_conv1_w"].T),
        "conv2_w": halves(get["L0_attn_conv2_w"].T),
        "dft": np.concatenate([halves(np.cos(angle).astype(np.float32)), halves(np.sin(angle).astype(np.float32))], 1),
        "freq": np.concatenate([halves(get[n][order][:, order]) for n in ("L0_ffn_w_freq_real", "L0_ffn_w_freq_imag")], 1),
    }
    nc = bacc.Bacc("TRN2", target_bir_lowering=False, num_devices=1)
    aps = {n: nc.dram_tensor(n, a.shape, F32, kind="ExternalInput").ap() for n, a in arrays.items()}
    out = nc.dram_tensor("out", (CH, P, B * T), F32, kind="ExternalOutput").ap()
    build(nc, out=out, **aps)
    result = run_bass_kernel_spmd(nc, [arrays], core_ids=[0])
    return np.ascontiguousarray(result.results[0]["out"].reshape(C, B, T).transpose(1, 2, 0))
```
